# Optimizing a Trainium2 kernel written in Bass

```python
import numpy as np
import jax
import jax.numpy as jnp

def _softmax(x, axis=-1):
    return jax.nn.softmax(x, axis=axis)

def _gelu(x):
    return jax.nn.gelu(x, approximate=True)

def _silu(x):
    return jax.nn.silu(x)

def _sigmoid(x):
    return jax.nn.sigmoid(x)

def _layernorm(x, axis=-1, eps=1e-05):
    m = jnp.mean(x, axis=axis, keepdims=True)
    v = jnp.var(x, axis=axis, keepdims=True)
    return (x - m) / jnp.sqrt(v + eps)

def _scatter_add(tgt, idx, src, axis=0):
    return tgt.at[idx].add(src)

def _segment_sum(src, seg, n):
    return jax.ops.segment_sum(src, seg, n)
kernel_name = 'mk_prb_d1_jaxref_r8_88ab10'

def setup_inputs(seed: int=0):
    np.random.seed(seed)
    _w = jnp.asarray

    def _L0_attn_setup():
        import jax, jax.numpy as jnp
        import numpy as np
        N_HEAD = 16
        D_MODEL = 256
        key = jax.random.key(seed)
        ks = jax.random.split(key, 9)
        B, T, C = (2, 256, D_MODEL)
        s = 1.0 / np.sqrt(C)
        return {'idx': jax.random.normal(ks[0], (B, T, C), dtype=jnp.float32), 'Wq': jax.random.normal(ks[1], (C, C), dtype=jnp.float32) * s, 'bq': jnp.zeros((C,), dtype=jnp.float32), 'Wk': jax.random.normal(ks[2], (C, C), dtype=jnp.float32) * s, 'bk': jnp.zeros((C,), dtype=jnp.float32), 'Wv': jax.random.normal(ks[3], (C, C), dtype=jnp.float32) * s, 'bv': jnp.zeros((C,), dtype=jnp.float32), 'Wo': jax.random.normal(ks[4], (C, C), dtype=jnp.float32) * s, 'bo': jnp.zeros((C,), dtype=jnp.float32)}
    _L0_attn_in = _L0_attn_setup()

    def _L0_ffn_setup():
        import jax, jax.numpy as jnp
        import numpy as np
        NUM_EXPERTS = 8
        TOP_K = 2
        HIDDEN = 256
        INTER = 256
        SWIGLU_LIMIT = 7.0
        BATCH, SEQ = (4, 256)
        key = jax.random.key(seed)
        k0, k1, k2, k3, k4 = jax.random.split(key, 5)
        x = jax.random.normal(k0, (BATCH, SEQ, HIDDEN), jnp.float32)
        Wr = jax.random.normal(k1, (HIDDEN, NUM_EXPERTS), jnp.float32) * 0.02
        Wg = jax.random.normal(k2, (NUM_EXPERTS, HIDDEN, INTER), jnp.float32) * 0.02
        Wu = jax.random.normal(k3, (NUM_EXPERTS, HIDDEN, INTER), jnp.float32) * 0.02
        Wd = jax.random.normal(k4, (NUM_EXPERTS, INTER, HIDDEN), jnp.float32) * 0.02
        return {'hidden_states': x, 'Wr': Wr, 'Wg': Wg, 'Wu': Wu, 'Wd': Wd}
    _L0_ffn_in = _L0_ffn_setup()
    _d = {'L0_attn_idx': _L0_attn_in['idx'], 'L0_attn_Wq': _L0_attn_in['Wq'], 'L0_attn_bq': _L0_attn_in['bq'], 'L0_attn_Wk': _L0_attn_in['Wk'], 'L0_attn_bk': _L0_attn_in['bk'], 'L0_attn_Wv': _L0_attn_in['Wv'], 'L0_attn_bv': _L0_attn_in['bv'], 'L0_attn_Wo': _L0_attn_in['Wo'], 'L0_attn_bo': _L0_attn_in['bo'], 'L0_ffn_Wr': _L0_ffn_in['Wr'], 'L0_ffn_Wg': _L0_ffn_in['Wg'], 'L0_ffn_Wu': _L0_ffn_in['Wu'], 'L0_ffn_Wd': _L0_ffn_in['Wd']}
    _x0 = _d['L0_attn_idx']
    _d['L0_attn_idx'] = jax.random.normal(jax.random.fold_in(jax.random.key(seed), 1), (4, 1024, 256), dtype=_x0.dtype)
    del _x0
    return _d

def reference(L0_attn_idx, L0_attn_Wq, L0_attn_bq, L0_attn_Wk, L0_attn_bk, L0_attn_Wv, L0_attn_bv, L0_attn_Wo, L0_attn_bo, L0_ffn_Wr, L0_ffn_Wg, L0_ffn_Wu, L0_ffn_Wd):

    def _L0_attn_ref(idx, Wq, bq, Wk, bk, Wv, bv, Wo, bo):
        import jax, jax.numpy as jnp
        import numpy as np
        N_HEAD = 16
        D_MODEL = 256
        B, T, C = idx.shape
        hs = C // N_HEAD

        def split_heads(x):
            return x.reshape(B, T, N_HEAD, hs).transpose(0, 2, 1, 3)
        q = split_heads(idx @ Wq + bq)
        k = split_heads(idx @ Wk + bk)
        v = split_heads(idx @ Wv + bv)
        scale = 1.0 / jnp.sqrt(jnp.asarray(hs, dtype=idx.dtype))
        scores = jnp.einsum('bhqd,bhkd->bhqk', q, k) * scale
        causal = jnp.tril(jnp.ones((T, T), dtype=bool))
        scores = jnp.where(causal, scores, -jnp.inf)
        attn = jax.nn.softmax(scores, axis=-1)
        out = jnp.einsum('bhqk,bhkd->bhqd', attn, v)
        out = out.transpose(0, 2, 1, 3).reshape(B, T, C)
        return out @ Wo + bo

    def _L0_ffn_ref(hidden_states, Wr, Wg, Wu, Wd):
        import jax, jax.numpy as jnp
        import numpy as np
        NUM_EXPERTS = 8
        TOP_K = 2
        HIDDEN = 256
        INTER = 256
        SWIGLU_LIMIT = 7.0
        BATCH, SEQ = (4, 256)
        router_logits = jnp.einsum('bsh,he->bse', hidden_states, Wr)
        topk_logits, selected = jax.lax.top_k(router_logits, TOP_K)
        router_probs = jax.nn.softmax(topk_logits, axis=-1)
        out = jnp.zeros_like(hidden_states)
        for e in range(NUM_EXPERTS):
            w_e = jnp.where(selected == e, router_probs, 0.0).sum(axis=-1, keepdims=True)
            g = jnp.einsum('bsh,hi->bsi', hidden_states, Wg[e])
            g = jnp.clip(jax.nn.silu(g), -SWIGLU_LIMIT, SWIGLU_LIMIT)
            u = jnp.einsum('bsh,hi->bsi', hidden_states, Wu[e])
            h = jnp.einsum('bsi,ih->bsh', g * u, Wd[e])
            out = out + h * w_e
        return out
    x = L0_attn_idx
    xn = _layernorm(x, axis=-1)
    x = x + _L0_attn_ref(xn, L0_attn_Wq, L0_attn_bq, L0_attn_Wk, L0_attn_bk, L0_attn_Wv, L0_attn_bv, L0_attn_Wo, L0_attn_bo) + _L0_ffn_ref(xn, L0_ffn_Wr, L0_ffn_Wg, L0_ffn_Wu, L0_ffn_Wd)
    return x

_drawn_inputs = setup_inputs


def setup_inputs(seed=0):
    import zlib

    import numpy as np

    out = dict(_drawn_inputs(seed))
    spreads = {'L0_attn_bq': (0.0, 0.72),
     'L0_attn_bk': (0.0, 0.8),
     'L0_attn_bv': (0.0, 0.1),
     'L0_attn_bo': (0.0, 0.1)}
    factors = {'L0_ffn_Wr': 5.54, 'L0_ffn_Wg': 4.828, 'L0_ffn_Wu': 4.769, 'L0_ffn_Wd': 4.777}
    for name, (base, spread) in spreads.items():
        noise = np.random.default_rng([zlib.crc32(name.encode()), seed]).standard_normal(out[name].shape)
        drawn = base * np.exp(spread * noise) if base else spread * noise
        out[name] = jnp.asarray(drawn.astype(out[name].dtype))
    for name, factor in factors.items():
        out[name] = (out[name] * factor).astype(out[name].dtype)
    return out
```

```python
from contextlib import ExitStack

import numpy as np
import concourse.bass as bass
from concourse import mybir

F32 = mybir.dt.float32
F32R = mybir.dt.float32r
BF16 = mybir.dt.bfloat16
U32 = mybir.dt.uint32
ACT = mybir.ActivationFunctionType
ALU = mybir.AluOpType
AX = mybir.AxisListType

P = 128
B, T, C = 4, 1024, 256
H, D = 16, 16
E, I = 8, 256
EPS = 1e-5
LIMIT = 7.0
MASKED = -1e30

KC = C // P
TILES = B * T // P
SUP = 4
SW = SUP * P
NSUP = TILES // SUP
HG = 4
NG = H // HG
GROUPS = B * NG
GC = HG * D
QT = T // P
SCALE = 1.0 / D ** 0.5
VW = 32

Q_PARTS = [0, 0, 0, 1, 1, 2]
K_PARTS = [0, 1, 2, 0, 1, 0]
PR = D * len(Q_PARTS)
SR = PR + 3
STACKS = NG


MOE_UNROLL = 4
MOE_TILES = -(-((2 * B * T + E * (P - 1)) // P) // MOE_UNROLL) * MOE_UNROLL
ZERO_TILES = 8


def wait(engine, semaphore, value):
    if isinstance(value, int) and value <= 0:
        return
    engine.wait_ge(semaphore, value)


def wait_alone(engine, semaphore, value, passed):
    if isinstance(value, int) and value <= 0:
        return
    engine.wait_ge(semaphore, value)
    engine.sem_inc(passed, 1)


def semaphores(nc, stack, names):
    return [stack.enter_context(nc.semaphore(n)) for n in names.split()]


def setup_phase(nc, m, a):
    with ExitStack() as stack:
        w_raw = stack.enter_context(nc.sbuf_tensor("w_raw", [P, KC, 4 * C + E], F32))
        loaded, built, hi_ready, lo_ready = semaphores(
            nc, stack, "weights_loaded constants_built weights_hi weights_lo")
        block = stack.enter_context(nc.Block())
        rows = lambda w: w.rearrange("(k p) c -> p k c", p=P)

        @block.sync
        def _(sp):
            for w, at in ((a["Wq"], 0), (a["Wk"], C), (a["Wv"], 2 * C), (a["Wr"], 3 * C), (a["Wo"], 3 * C + E)):
                sp.dma_start(w_raw[:, :, at:at + w.shape[1]], rows(w)).then_inc(loaded, 16)
            for n, v in enumerate((a["bq"], a["bk"])):
                sp.dma_start(m["qk_bias"][:, n, :], v.rearrange("(k p) -> p k", p=P),
                             allow_slow_non_contiguous=True).then_inc(loaded, 16)
            for n, v in enumerate((a["bv"], a["bo"])):
                sp.dma_start(m["row_bias"][:, n, :], v.rearrange("(o c) -> o c", o=1).broadcast_to([P, C])).then_inc(loaded, 16)

        @block.scalar
        def _(act):
            act.wait_ge(loaded, 16 * 9)
            nc.scalar.activation(m["w_hi"][:], w_raw[:], ACT.Copy).then_inc(hi_ready, 1)
            act.wait_ge(lo_ready, 1)

        @block.vector
        def _(dve):
            nc.vector.memset(m["eps"][:], EPS)
            dve.wait_ge(hi_ready, 1)
            nc.vector.tensor_tensor(m["w_lo"][:], w_raw[:], m["w_hi"][:].bitcast(F32), ALU.subtract).then_inc(lo_ready, 1)

        @block.gpsimd
        def _(pool):
            zeros = nc.gpsimd.memset(m["ident"][:], 0.0)
            nc.gpsimd.memset(m["ident_b"][:], 0.0)
            nc.gpsimd.memset(m["mask_b"][:], 0.0).then_inc(built, 1)
            pool.wait_ge(built, 1)
            for t in (m["ident"], m["ident_b"]):
                nc.gpsimd.affine_select(out=t[:], in_=t[:], compare_op=ALU.not_equal, fill=1.0, base=0,
                                        pattern=[[-1, P]], channel_multiplier=1)
            nc.gpsimd.affine_select(out=m["mask_b"][:], in_=m["mask_b"][:], compare_op=ALU.is_ge, fill=MASKED,
                                    base=0, pattern=[[-1, P]], channel_multiplier=1)
            for par in range(2):
                nc.gpsimd.memset(m["v_ext"][:, par], 0.0).then_inc(built, 1)
            pool.wait_ge(built, 3)
            for par in range(2):
                nc.gpsimd.memset(m["v_ext"][:, par, :, :, D:D + 1], 1.0).then_inc(built, 1)


def project_phase(nc, m, x, xn_dram, parts_dram, slots_dram):
    with ExitStack() as stack:
        sb = lambda name, shape, dt=F32: stack.enter_context(nc.sbuf_tensor(name, shape, dt))
        ps = lambda name, shape: stack.enter_context(nc.psum_tensor(name, shape, F32))
        x_all, xn = sb("x_all", [P, NSUP, SUP, C]), sb("xn", [P, 2, SUP, C])
        xt_hi, xt_lo = sb("xt_hi", [P, 2, KC, SW], F32R), sb("xt_lo", [P, 2, KC, SW], F32R)
        part, rest = sb("part", [P, 2, 3, 2, KC, SW], BF16), sb("rest", [P, 2, 2, KC, SW])
        stats, mv = sb("stats", [P, SUP, 6]), sb("mv", [P, 2, SUP, 2])
        std, rstd = sb("std", [P, 2, SUP]), sb("rstd", [P, 2, SUP])
        ps_xt, ps_qk, ps_v = ps("ps_xt", [P, KC, SW]), ps("ps_qk", [P, 2, KC, SW]), ps("ps_v", [P, 2, 512])
        (stats_ready, mv_ready, std_ready, rstd_ready, xn_ready, xt_in_psum, hi_ready, lo_ready, qk_in_psum,
         part0_ready, rest_ready, part1_ready, part2_ready, v_in_psum, v_ready) = semaphores(
            nc, stack, "stats_ready mv_ready std_ready rstd_ready xn_ready xt_in_psum hi_ready lo_ready qk_in_psum "
            "part0_ready rest_ready part1_ready part2_ready v_in_psum v_ready")
        zeros = sb("zeros", [P, ZERO_TILES * C])
        zeros_ready, zeroed = semaphores(nc, stack, "zeros_ready zeroed")
        x_loaded = semaphores(nc, stack, "x_loaded_even x_loaded_odd")
        xn_stored = semaphores(nc, stack, "xn_stored_even xn_stored_odd")
        stored = semaphores(nc, stack, "parts_stored_even parts_stored_odd")
        block = stack.enter_context(nc.Block())
        x_view = x.rearrange("b (n j p) c -> p (b n) j c", p=P, j=SUP)
        xn_view = xn_dram.rearrange("(n j p) c -> p n j c", p=P, j=SUP)
        parts_view = parts_dram.rearrange("r a b (k p) (h t) -> r a k h p b t", p=P, t=SW)
        units = [(q, k) for q in range(2) for k in range(KC)]
        PARTS_STORED = 16 * 3 * len(units)

        def rounds(engine, body):
            body(0, False)
            with engine.Fori(1, NSUP // 2 - 1) as it:
                body(it, False)
            body(NSUP // 2 - 1, True)

        @block.sync
        def _(sp):
            for n in range(NSUP):
                wait(sp, x_loaded[n % 2], 16 * (n // 2))
                sp.dma_start(x_all[:, n], x_view[:, n]).then_inc(x_loaded[n % 2], 16)

            def body(it, last):
                for par in range(2):
                    n = 2 * it + par
                    wait(sp, xn_ready, n + 1)
                    sp.dma_start(xn_view[:, bass.ds(n, 1)], xn[:, par:par + 1]).then_inc(xn_stored[par], 16)
                    wait(sp, part2_ready, 4 * (n + 1))
                    for r in range(3):
                        for q, k in units:
                            sp.dma_start(parts_view[r, q, k, par][:, bass.ds(it, 1)],
                                         part[:, par, r, q, k].rearrange("p (o t) -> p o t", o=1)).then_inc(stored[par], 16)
            rounds(sp, body)
            for par in range(2):
                sp.wait_ge(xn_stored[par], 16 * NSUP // 2)
                sp.wait_ge(stored[par], PARTS_STORED * NSUP // 2)

        def root(n, par):
            nc.scalar.wait_ge(mv_ready, n + 1)
            nc.scalar.activation(std[:, par], mv[:, par, :, 1], ACT.Sqrt, bias=m["eps"][:, 0:1]).then_inc(std_ready, 1)

        @block.scalar
        def _(act):
            def hi(n, par):
                act.wait_ge(xt_in_psum, n + 1)
                wait(act, v_in_psum, SUP * (n - 1))
                nc.scalar.activation(xt_hi[:, par], ps_xt[:], ACT.Copy).then_inc(hi_ready, 1)

            def body(it, last):
                for par in range(2):
                    n = 2 * it + par
                    if not last:
                        root(n + 2, par)
                    if not (last and par):
                        hi(n + 1, 1 - par)
                    for u, (q, k) in enumerate(units):
                        act.wait_ge(qk_in_psum, 4 * n + u + 1)
                        wait(act, stored[par], PARTS_STORED * it)
                        nc.scalar.activation(part[:, par, 0, q, k], ps_qk[:, q, k], ACT.Identity,
                                             bias=m["qk_bias"][:, q, k:k + 1]).then_inc(part0_ready, 1)
            root(0, 0)
            root(1, 1)
            hi(0, 0)
            rounds(act, body)

        @block.vector
        def _(dve):
            def moments(n, par, it):
                dve.wait_ge(x_loaded[par], 16 * (it + 1))
                wait(dve, mv_ready, n)
                for j in range(SUP):
                    last = nc.vector.bn_stats(stats[:, j], x_all[:, n, j])
                last.then_inc(stats_ready, 1)
                wait_alone(dve, stats_ready, n + 1, m["passed"])
                for j in range(SUP):
                    last = nc.vector.bn_aggr(mv[:, par, j], stats[:, j])
                last.then_inc(mv_ready, 1)

            def normalise(n, par, it):
                dve.wait_ge(std_ready, n + 1)
                nc.vector.reciprocal(rstd[:, par], std[:, par]).then_inc(rstd_ready, 1)
                dve.wait_ge(rstd_ready, n + 1)
                wait(dve, xt_in_psum, n - 1)
                wait(dve, xn_stored[par], 16 * it)
                for j in range(SUP):
                    last = nc.vector.tensor_scalar(xn[:, par, j],
                                                   x_all[:, n, j],
                                                   mv[:, par, j, 0:1], rstd[:, par, j:j + 1], ALU.subtract, ALU.mult)
                last.then_inc(xn_ready, 1)

            def lo(n, par):
                dve.wait_ge(hi_ready, n + 1)
                nc.vector.tensor_tensor(xt_lo[:, par], ps_xt[:], xt_hi[:, par].bitcast(F32), ALU.subtract).then_inc(lo_ready, 1)

            def body(it, last):
                for par in range(2):
                    n = 2 * it + par
                    if not last:
                        moments(n + 2, par, it + 1)
                    if not (last and par):
                        lo(n + 1, 1 - par)
                    if not last:
                        normalise(n + 2, par, it + 1)
                    for u, (q, k) in enumerate(units):
                        dve.wait_ge(part0_ready, 4 * n + u + 1)
                        wait(dve, part2_ready, 4 * (n - 1))
                        nc.vector.scalar_tensor_tensor(out=rest[:, par, q, k], in0=ps_qk[:, q, k],
                                                       scalar=m["qk_bias"][:, q, k:k + 1], in1=part[:, par, 0, q, k],
                                                       op0=ALU.add, op1=ALU.subtract).then_inc(rest_ready, 1)
                    for j in range(SUP):
                        dve.wait_ge(v_in_psum, SUP * n + j + 1)
                        nc.vector.tensor_tensor(
                            m["v_all"][:, bass.ds(NG * it, NG), SUP * par + j, :],
                            ps_v[:, j % 2, :C].rearrange("p (g c) -> p g c", g=NG),
                            m["row_bias"][:, 0].rearrange("p (g c) -> p g c", g=NG), ALU.add)
                        nc.vector.tensor_copy(m["logits"][:, SUP * n + j],
                                              ps_v[:, j % 2, C:C + E]).then_inc(v_ready, 1)
            for n in range(2):
                moments(n, n, 0)
            for n in range(2):
                normalise(n, n, 0)
            lo(0, 0)
            rounds(dve, body)

        @block.gpsimd
        def _(pool):
            nc.gpsimd.memset(zeros[:], 0.0).then_inc(zeros_ready, 1)
            pool.wait_ge(zeros_ready, 1)
            with pool.Fori(0, MOE_TILES // ZERO_TILES) as i:
                pool.dma_start(slots_dram.rearrange("(i p j) c -> p i (j c)", p=P, j=ZERO_TILES)[:, bass.ds(i, 1)],
                               zeros[:].rearrange("p (o w) -> p o w", o=1)).then_inc(zeroed, 16)

            def body(it, last):
                for par in range(2):
                    n = 2 * it + par
                    wait(pool, stored[par], PARTS_STORED * it)
                    for u, (q, k) in enumerate(units):
                        wait_alone(pool, rest_ready, 4 * n + u + 1, m["passed"])
                        nc.gpsimd.tensor_copy(part[:, par, 1, q, k], rest[:, par, q, k]).then_inc(part1_ready, 1)
                        pool.wait_ge(part1_ready, 4 * n + u + 1)
                        nc.gpsimd.tensor_tensor(part[:, par, 2, q, k], rest[:, par, q, k], part[:, par, 1, q, k],
                                                ALU.subtract).then_inc(part2_ready, 1)
            rounds(pool, body)
            pool.wait_ge(zeroed, 16 * (MOE_TILES // ZERO_TILES))

        @block.tensor
        def _(pe):
            passes = lambda par: ((m["w_hi"], xt_hi), (m["w_hi"], xt_lo), (m["w_lo"], xt_hi))

            def transposes(n, par):
                pe.wait_ge(xn_ready, n + 1)
                wait(pe, lo_ready, n)
                for j in range(SUP):
                    for k in range(KC):
                        last = nc.tensor.transpose(
                            ps_xt[:, k, j * P:(j + 1) * P],
                            xn[:, par, j, k * P:(k + 1) * P], m["ident"][:])
                last.then_inc(xt_in_psum, 1)

            def body(it, last):
                for par in range(2):
                    n = 2 * it + par
                    if not (last and par):
                        transposes(n + 1, 1 - par)
                    pe.wait_ge(lo_ready, n + 1)
                    for u, (q, k) in enumerate(units):
                        wait(pe, rest_ready, 4 * n + u - 3)
                        terms = [(w, v, c) for c in range(KC) for w, v in passes(par)]
                        for i, (w, v, c) in enumerate(terms):
                            last_mm = nc.tensor.matmul(ps_qk[:, q, k], w[:, c, q * C + k * P:q * C + (k + 1) * P],
                                                       v[:, par, c], start=(i == 0), stop=(i == len(terms) - 1))
                        last_mm.then_inc(qk_in_psum, 1)
                    for j in range(SUP):
                        wait(pe, v_ready, SUP * n + j - 1)
                        for i, (w, v, c) in enumerate(terms):
                            last_mm = nc.tensor.matmul(ps_v[:, j % 2, :C + E], v[:, par, c, j * P:(j + 1) * P],
                                                       w[:, c, 2 * C:3 * C + E], start=(i == 0), stop=(i == len(terms) - 1))
                        last_mm.then_inc(v_in_psum, 1)
            transposes(0, 0)
            rounds(pe, body)




def route_phase(nc, m):
    with ExitStack() as stack:
        sb = lambda name, shape, dt=F32: stack.enter_context(nc.sbuf_tensor(name, shape, dt))
        ps = lambda name, shape: stack.enter_context(nc.psum_tensor(name, shape, F32))
        cell = [P, TILES, E]
        order, left, first, second, t0 = (sb(n, cell) for n in ("order", "left", "first", "second", "t0"))
        top1, top2, pick, gap, total = (sb(n, [P, TILES]) for n in ("top1", "top2", "pick", "gap", "total"))
        chosen, upper, ones = sb("chosen", cell, BF16), sb("upper", [P, P], BF16), sb("ones", [P, P], BF16)
        scan = sb("scan", [P, 2, TILES, E])
        need, need_int, start = sb("need", [P, E]), sb("need_int", [P, E], mybir.dt.int32), sb("start", [P, 4, E])
        number, owner = sb("number", [P, MOE_TILES, E]), sb("owners", [P, MOE_TILES])
        ps_rank, ps_count = ps("ps_rank", cell), ps("ps_count", cell)
        step, built, made, exp_ready, gap_ready, chosen_ready, counted = semaphores(
            nc, stack, "route_step built made exp_ready gap_ready chosen_ready counted")
        block = stack.enter_context(nc.Block())
        per_tile = lambda v: v.rearrange("p (t o) -> p t o", o=1).broadcast_to(cell)
        per_expert = lambda v, n: v.rearrange("p (o e) -> p o e", o=1).broadcast_to([P, n, E])

        @block.gpsimd
        def _(pool):
            nc.gpsimd.iota(order[:], [[0, TILES], [-1, E]], base=E, channel_multiplier=0,
                           allow_small_or_imprecise_dtypes=True).then_inc(built, 1)
            nc.gpsimd.iota(number[:], [[1, MOE_TILES], [0, E]], base=0, channel_multiplier=0,
                           allow_small_or_imprecise_dtypes=True).then_inc(built, 1)
            nc.gpsimd.memset(ones[:], 1.0).then_inc(built, 1)
            pool.wait_ge(built, 3)
            nc.gpsimd.affine_select(out=upper[:], in_=ones[:], compare_op=ALU.is_gt, fill=0.0, base=0,
                                    pattern=[[1, P]], channel_multiplier=-1).then_inc(built, 1)

        @block.scalar
        def _(act):
            act.wait_ge(gap_ready, 1)
            nc.scalar.activation(gap[:], gap[:], ACT.Exp).then_inc(exp_ready, 1)

        @block.tensor
        def _(pe):
            pe.wait_ge(built, 4)
            pe.wait_ge(chosen_ready, 1)
            nc.tensor.matmul(ps_rank[:], upper[:], chosen[:], start=True, stop=True)
            nc.tensor.matmul(ps_count[:], ones[:], chosen[:], start=True, stop=True).then_inc(counted, 1)

        @block.vector
        def _(dve):
            chain = [0]

            def link(ins):
                chain[0] += 1
                ins.then_inc(step, 1)
                dve.wait_ge(step, chain[0])
            tt, ts = nc.vector.tensor_tensor, nc.vector.tensor_scalar
            logits = m["logits"][:]

            def best(scores, top, mark):
                link(nc.vector.tensor_reduce(top[:], scores, AX.X, ALU.max))
                link(tt(t0[:], scores, per_tile(top[:]), ALU.is_equal))
                link(tt(t0[:], t0[:], order[:], ALU.mult))
                link(nc.vector.tensor_reduce(pick[:], t0[:], AX.X, ALU.max))
                link(tt(mark[:], t0[:], per_tile(pick[:]), ALU.is_equal))
            dve.wait_ge(built, 4)
            best(logits, top1, first)
            link(ts(left[:], first[:], MASKED, None, ALU.mult))
            link(tt(left[:], left[:], logits, ALU.add))
            best(left[:], top2, second)
            tt(chosen[:], first[:], second[:], ALU.add).then_inc(chosen_ready, 1)
            tt(gap[:], top2[:], top1[:], ALU.subtract).then_inc(gap_ready, 1)
            dve.wait_ge(exp_ready, 1)
            link(ts(total[:], gap[:], 1.0, None, ALU.add))
            link(nc.vector.reciprocal(m["weight"][:, 0], total[:]))
            link(tt(m["weight"][:, 1], gap[:], m["weight"][:, 0], ALU.mult))

            dve.wait_ge(counted, 1)
            link(nc.vector.tensor_copy(scan[:, 0], ps_count[:]))
            at, shift = 0, 1
            while shift < TILES:
                nc.vector.tensor_copy(scan[:, 1 - at, :shift], scan[:, at, :shift])
                link(tt(scan[:, 1 - at, shift:], scan[:, at, shift:], scan[:, at, :TILES - shift], ALU.add))
                at, shift = 1 - at, 2 * shift
            incl = scan[:, at]
            link(ts(need[:], incl[:, TILES - 1], 1.0 / P, (P - 1.0) / P - 0.498, ALU.mult, ALU.add))
            link(nc.vector.tensor_copy(need_int[:], need[:]))
            link(nc.vector.tensor_copy(need[:], need_int[:]))
            link(nc.vector.memset(start[:, 0], 0.0))
            link(nc.vector.tensor_copy(start[:, 0, 1:], need[:, :E - 1]))
            for n, shift in enumerate((1, 2, 4)):
                nc.vector.tensor_copy(start[:, n + 1, :shift], start[:, n, :shift])
                link(tt(start[:, n + 1, shift:], start[:, n, shift:], start[:, n, :E - shift], ALU.add))
            link(tt(t0[:], incl, ps_count[:], ALU.subtract))
            link(tt(t0[:], t0[:], ps_rank[:], ALU.add))
            link(ts(need[:], start[:, 3], float(P), None, ALU.mult))
            link(tt(t0[:], t0[:], per_expert(need[:], TILES), ALU.add))
            for n, mark in enumerate((first, second)):
                link(tt(left[:], t0[:], mark[:], ALU.mult))
                link(nc.vector.tensor_reduce(total[:], left[:], AX.X, ALU.add))
                link(nc.vector.tensor_copy(m["slot"][:, n], total[:]))
            link(tt(number[:], per_expert(start[:, 3], MOE_TILES), number[:], ALU.is_le))
            link(nc.vector.tensor_reduce(owner[:], number[:, :, 1:], AX.X, ALU.add))
            link(nc.vector.tensor_copy(m["owner"][:], owner[:]))


STEPS = [(half, i) for half in range(2) for i in range(4 * (half + 1))]
DIAGONAL = [s for s, (half, i) in enumerate(STEPS) if i >= 4 * half]
LAG = 2
P_SETS = 3
S_BANKS = 3
MAX_UNITS = [(j, h, n) for j in range(QT) for n in (4 if j < 2 else 2 if j < 4 else 1,) for h in range(0, HG, n)]
AHEAD = 3
RING = ([("max", 1, u) for u in range(AHEAD, 14)] + [("rows", 0, 0)]
        + [("max", 1, u) for u in range(14, len(MAX_UNITS))] + [("turn", 1, 0)]
        + [("max", 2, u) for u in range(AHEAD)] + [("rows", 0, 1)])
BEFORE_ROWS = RING.index(("rows", 0, 0))
ROWS_PLACE = 14
RING_PLACE = {r: "end" for r in RING}
for v, r in enumerate(RING[:RING.index(("turn", 1, 0))]):
    v += ROWS_PLACE - BEFORE_ROWS if v >= BEFORE_ROWS else 0
    RING_PLACE[r] = (v // 2, 2 * (v % 2) + 1)
RING_PLACE["turn", 1, 0] = (len(STEPS) - 1, HG - 1)
FIRST_RING = [("max", 0, u) for u in range(len(MAX_UNITS))] + [("turn", 0, 0)] + [("max", 1, u) for u in range(AHEAD)]


def attention_phase(nc, m, parts_dram, xn_dram, slots_dram):
    with ExitStack() as stack:
        sb = lambda name, shape, dt=F32: stack.enter_context(nc.sbuf_tensor(name, shape, dt))
        ps = lambda name, shape: stack.enter_context(nc.psum_tensor(name, shape, F32))
        prob, heads_out = sb("prob", [P, P_SETS, HG, SW]), sb("heads_out", [P, 2, SW])
        neg_max, max_part = sb("neg_max", [P, 2, HG, QT]), sb("max_part", [HG * QT, 2, 3, P], BF16)
        max_rest, recip = sb("max_rest", [HG * QT, 2, P]), sb("recip", [P, 2, 4, HG])
        ps_ring, ps_s, ps_o = ps("ps_ring", [P, 2, 1024]), ps("ps_s", [P, S_BANKS, SW]), ps("ps_o", [P, SW])
        (scores_done, exp_done, masked, values_done, ring_done, ring_free, split, split_ready, copied, recip_ready,
         v_ready, ones_ready) = semaphores(nc, stack, "scores_done exp_done masked values_done ring_done ring_free "
                               "split split_ready heads_copied recip_ready v_ext_ready ones_ready")
        loaded = semaphores(nc, stack, "stack_loaded_even stack_loaded_odd")
        max_loaded = semaphores(nc, stack, "max_loaded_even max_loaded_odd")
        rows, row_slot = sb("rows", [P, 2, 2, C]), sb("row_slot", [P, 2, 2, 2], U32)
        rows_loaded = semaphores(nc, stack, "rows_loaded_even rows_loaded_odd")
        scattered = semaphores(nc, stack, "scattered_even scattered_odd")
        slot_copied, rows_free = semaphores(nc, stack, "slot_copied rows_free")
        rows_view = xn_dram.rearrange("(n j p) c -> p n j c", p=P, j=2)
        block = stack.enter_context(nc.Block())
        q_stack, k_stack, v_ext, attn = m["q_stack"], m["k_stack"], m["v_ext"], m["attn"]
        view = parts_dram.rearrange("r a b (g h d) t -> a r (b g) d h t", g=NG, d=D)
        LOADS = 16 * 2 * len(Q_PARTS)
        NS = len(STEPS)

        def rounds(engine, body):
            with engine.Fori(0, B - 1) as it:
                for g in range(NG):
                    body(NG * it + g, it, g, False)
            for g in range(NG):
                body(NG * (B - 1) + g, B - 1, g, True)

        def group_pairs(it, g):
            return NG // 2 * it + g // 2

        def ring_units(it, g, last):
            before = len(FIRST_RING) + len(RING) * (NG * it + g)
            units = RING
            if last:
                units = [r for r in RING if g + r[1] < NG]
                before -= sum(q + r[1] >= NG for q in range(g) for r in RING)
            start = (len(FIRST_RING) + len(RING) * g - (sum(q + r[1] >= NG for q in range(g) for r in RING) if last else 0)) % 2
            return [(r, before + v, (start + v) % 2) for v, r in enumerate(units)]

        def score_bank(s, h):
            return (HG * s + h) % S_BANKS

        def width(s):
            half, i = STEPS[s]
            first = max(SW * half, P * i)
            return first, SW * (half + 1) - first

        @block.sync
        def _(sp):
            def load(n, g, buf):
                for which, (stk, parts) in enumerate(((q_stack, Q_PARTS), (k_stack, K_PARTS))):
                    for r, part in enumerate(parts):
                        sp.dma_start(stk[D * r:D * (r + 1), buf], view[which, part, n]).then_inc(loaded[g % 2], 16)

            def max_rows(k2, g):
                sp.wait_ge(split_ready, k2)
                for r in range(3):
                    sp.dma_start(q_stack[PR + r:PR + r + 1, g % STACKS].rearrange("o h (j t) -> o (h j) t", t=P),
                                 max_part[:, g % 2, r]).then_inc(max_loaded[g % 2], 16)
            def load_rows(n, it, g):
                wait_alone(sp, rows_free, n + 1, m["passed"])
                sp.dma_start(rows[:, g % 2:g % 2 + 1], rows_view[:, bass.ds(n, 1)]).then_inc(rows_loaded[g % 2], 16)
            for n in range(2):
                load(n, n, n)
            load_rows(0, 0, 0)
            max_rows(1, 0)

            def body(n, it, g, last):
                if not (last and g + 2 >= NG):
                    sp.wait_ge(scores_done, len(STEPS) * HG * n + 1)
                    load(n + 2, g, (g + 2) % STACKS)
                if not (last and g + 1 >= NG):
                    load_rows(n + 1, it, g + 1)
                    max_rows(n + 2, g + 1)
            rounds(sp, body)

        @block.gpsimd
        def _(pool):
            def values(n, g):
                nc.gpsimd.tensor_copy(v_ext[:, g % 2, :, :, :D],
                                      m["v_all"][:, n].rearrange("p k (h d) -> p k h d", h=HG)).then_inc(v_ready, 1)
            values(0, 0)
            pool.sem_inc(rows_free, 2)

            def scatter(n, it, g):
                nc.gpsimd.tensor_copy(row_slot[:, g % 2], m["slot"][:, :, bass.ds(2 * n, 2)]).then_inc(slot_copied, 1)
                pool.wait_ge(slot_copied, n + 1)
                wait_alone(pool, rows_loaded[g % 2], 16 * (group_pairs(it, g) + 1), m["passed"])
                for j in range(2):
                    for which in range(2):
                        nc.gpsimd.indirect_dma_start(
                            slots_dram, bass.IndirectOffsetOnAxis(ap=row_slot[:, g % 2, which, j:j + 1], axis=0),
                            rows[:, g % 2, j], None).then_inc(scattered[g % 2], 16)

            def body(n, it, g, last):
                for d, s in enumerate(DIAGONAL):
                    wait_alone(pool, exp_done, S_BANKS + HG * (NS * n + s + 1), m["passed"])
                    block_ = prob[:, s % P_SETS, :, :P]
                    nc.gpsimd.affine_select(out=block_, in_=block_, compare_op=ALU.is_ge, fill=0.0, base=0,
                                            pattern=[[0, HG], [1, P]], channel_multiplier=-1).then_inc(masked, 1)
                    if d == 1 and not (last and g + 1 >= NG):
                        pool.wait_ge(values_done, P_SETS + NS * n)
                        values(n + 1, g + 1)
                    if d == 2:
                        scatter(n, it, g)
                wait_alone(pool, scattered[g % 2], 64 * (group_pairs(it, g) + 1), m["passed"])
                pool.sem_inc(rows_free, 1)
            rounds(pool, body)

        @block.scalar
        def _(act):
            act.sem_inc(exp_done, S_BANKS)
            act.sem_inc(copied, 1)

            def copy_out(n, g, half, at):
                act.wait_ge(values_done, P_SETS + NS * n + (4, NS)[half])
                act.wait_ge(ring_done, at - len(RING))
                nc.scalar.activation(heads_out[:, half], ps_o[:], ACT.Copy).then_inc(copied, 1)

            def body(n, it, g, last):
                for s in range(NS):
                    for h in range(HG):
                        _, w = width(s)
                        U = HG * (NS * n + s) + h
                        act.wait_ge(scores_done, U + 1)
                        if h == 0:
                            act.wait_ge(values_done, NS * n + s + 1)
                        nc.scalar.activation(prob[:, s % P_SETS, h, :w], ps_s[:, score_bank(s, h), :w], ACT.Exp,
                                             scale=SCALE).then_inc(exp_done, 1)
                        if (s, h) == (6, 0):
                            copy_out(n, g, 0, len(FIRST_RING) + len(RING) * n)
                copy_out(n, g, 1, len(FIRST_RING) + len(RING) * n)
            rounds(act, body)

        @block.vector
        def _(dve):
            nc.vector.memset(k_stack[PR:P], 1.0).then_inc(ones_ready, 1)

            def ring(unit, n, it, g, at, slot):
                kind, ahead, u = unit
                dve.wait_ge(ring_done, at + 1)
                gg = g + ahead
                if kind == "max":
                    j, h, heads = MAX_UNITS[u]
                    w = (j + 1) * P
                    stride = 1024 // heads if j else P
                    if heads == 2:
                        stride = 512
                    src = ps_ring[:, slot, :heads * stride].rearrange("p (h w) -> p h w", h=heads)[:, :, :w]
                    nc.vector.tensor_reduce(neg_max[:, gg % 2, h:h + heads, j], src, AX.X, ALU.max,
                                            negate=True).then_inc(ring_free, 1)
                elif kind == "turn":
                    src = ps_ring[:HG * QT, slot, :P]
                    mp, rest = max_part[:, gg % 2], max_rest[:, 0]
                    before = 4 * (n + ahead)
                    nc.vector.tensor_copy(mp[:, 0], src).then_inc(split, 1)
                    dve.wait_ge(split, before + 1)
                    nc.vector.tensor_tensor(rest, src, mp[:, 0], ALU.subtract).then_inc(split, 1)
                    dve.wait_ge(split, before + 2)
                    nc.vector.tensor_copy(mp[:, 1], rest).then_inc(split, 1)
                    dve.wait_ge(split, before + 3)
                    nc.vector.tensor_tensor(mp[:, 2], rest, mp[:, 1], ALU.subtract).then_inc(split, 1)
                    dve.wait_ge(split, before + 4)
                    dve.sem_inc(split_ready, 1)
                    dve.sem_inc(ring_free, 1)
                else:
                    src = ps_ring[:, slot, :SW].rearrange("p (j h v) -> p j h v", j=4, h=HG)
                    rc = recip[:, u]
                    nc.vector.reciprocal(rc, src[:, :, :, D]).then_inc(recip_ready, 1)
                    dve.wait_ge(recip_ready, 2 * n + u + 1)
                    dst = attn[:, g, bass.ds(QT * it + 4 * u, 4)].rearrange("p j (h d) -> p j h d", h=HG)
                    nc.vector.tensor_tensor(dst, src[:, :, :, :D], rc.rearrange("p j (h o) -> p j h o", o=1).broadcast_to([P, 4, HG, D]),
                                            ALU.mult).then_inc(ring_free, 1)

            for v, r in enumerate(FIRST_RING):
                ring(r, 0, 0, 0, v, v % 2)

            def body(n, it, g, last):
                for r, at, slot in ring_units(it, g, last):
                    ring(r, n, it, g, at, slot)
            rounds(dve, body)

        @block.tensor
        def _(pe):
            def ring(unit, n, it, g, at, slot):
                kind, ahead, u = unit
                gg = g + ahead
                if kind == "turn":
                    wait(pe, ring_free, at)
                    nc.tensor.transpose(ps_ring[:HG * QT, slot, :P], neg_max[:, gg % 2].rearrange("p h j -> p (h j)"),
                                        m["ident"][:]).then_inc(ring_done, 1)
                    return
                wait(pe, ring_free, at - 1)
                if kind == "rows":
                    pe.wait_ge(copied, 2 * n + u + 2)
                    for j in range(4):
                        last = nc.tensor.transpose(ps_ring[:, slot, P * j:P * (j + 1)],
                                                   heads_out[:, u, P * j:P * (j + 1)], m["ident"][:])
                    last.then_inc(ring_done, 1)
                    return
                j, h0, heads = MAX_UNITS[u]
                if u == 0:
                    pe.wait_ge(loaded[gg % 2], LOADS * (group_pairs(it, gg) + 1))
                buf = gg % STACKS
                stride = P if heads == 4 and j == 0 else 256 if heads == 4 else 512
                for hh in range(heads):
                    q = q_stack[:PR, buf, h0 + hh, P * j:P * (j + 1)]
                    w = (j + 1) * P
                    for c in range(0, w, SW):
                        cw = min(SW, w - c)
                        at_ = hh * stride + c
                        diagonal = c + cw == w
                        nc.tensor.matmul(ps_ring[:, slot, at_:at_ + cw], q, k_stack[:PR, buf, h0 + hh, c:c + cw],
                                         start=True, stop=not diagonal)
                    at_ = hh * stride + w - P
                    last = nc.tensor.matmul(ps_ring[:, slot, at_:at_ + P], m["ident_b"][:], m["mask_b"][:],
                                            start=False, stop=True)
                last.then_inc(ring_done, 1)

            for v, r in enumerate(FIRST_RING):
                ring(r, 0, 0, 0, v, v % 2)
            pe.wait_ge(ones_ready, 1)
            pe.sem_inc(values_done, P_SETS)

            def scores(n, it, g, s, h):
                half, i = STEPS[s]
                first, w = width(s)
                U = HG * (NS * n + s) + h
                if s == 0 and h == 0:
                    pe.wait_ge(max_loaded[g % 2], 48 * (group_pairs(it, g) + 1))
                pe.wait_ge(exp_done, U + 1)
                nc.tensor.matmul(ps_s[:, score_bank(s, h), :w], k_stack[:SR, g % STACKS, h, P * i:P * (i + 1)],
                                 q_stack[:SR, g % STACKS, h, first:first + w], start=True, stop=True).then_inc(scores_done, 1)

            def sums(n, g, s):
                half, i = STEPS[s]
                first, w = width(s)
                pe.wait_ge(exp_done, S_BANKS + HG * (NS * n + s + 1))
                if s in DIAGONAL:
                    pe.wait_ge(masked, len(DIAGONAL) * n + DIAGONAL.index(s) + 1)
                if i == 0:
                    pe.wait_ge(copied, 2 * n + half + 1)
                if s == 0:
                    pe.wait_ge(v_ready, n + 1)
                for h in range(HG):
                    last = nc.tensor.matmul(ps_o[VW * h:VW * (h + 1), first - SW * half:first - SW * half + w],
                                            v_ext[:, g % 2, i, h], prob[:, s % P_SETS, h, :w],
                                            start=(i == 0), stop=(s in (3, NS - 1)))
                last.then_inc(values_done, 1)

            def body(n, it, g, last):
                places = {}
                for r, at, slot in ring_units(it, g, last):
                    places.setdefault(RING_PLACE[r], []).append((r, at, slot))

                def ring_behind(place):
                    for r, at, slot in places.get(place, []):
                        ring(r, n, it, g, at, slot)
                for s in range(NS + LAG):
                    if s < NS:
                        for h in range(HG):
                            scores(n, it, g, s, h)
                            ring_behind((s, h))
                    if s >= LAG:
                        sums(n, g, s - LAG)
                ring_behind("end")
            rounds(pe, body)


def expert_phase(nc, m, a, slots_dram, y_dram):
    with ExitStack() as stack:
        sb = lambda name, shape, dt=F32: stack.enter_context(nc.sbuf_tensor(name, shape, dt))
        ps = lambda name, shape: stack.enter_context(nc.psum_tensor(name, shape, F32))
        W = 2 * I + C
        w_hi, w_lo, w_raw = sb("we_hi", [P, E, KC, W], F32R), sb("we_lo", [P, E, KC, W], F32R), sb("we_raw", [P, 2, KC, W])
        x_in, y_out = sb("slot_in", [P, MOE_UNROLL, C]), sb("slot_out", [P, MOE_UNROLL, C])
        xt_hi, xt_lo, ht_hi, ht_lo = (sb(n, [P, 2, KC, P], F32R) for n in ("sx_hi", "sx_lo", "sh_hi", "sh_lo"))
        gate, clipped, inner = (sb(n, [P, 2, I]) for n in ("gate", "clipped", "inner"))
        ps_xt, ps_gu, ps_ht, ps_y = (ps(n, [P, 2, 512]) for n in ("ps_sx", "ps_gu", "ps_sh", "ps_y"))
        (w_hi_ready, w_lo_ready, x_turned, x_hi, x_lo, gu_done, gate_ready, clip_ready, inner_ready, h_turned,
         h_hi, h_lo, y_done, y_copied) = semaphores(
            nc, stack, "we_hi_ready we_lo_ready x_turned x_hi x_lo gu_done gate_ready clip_ready inner_ready "
            "h_turned h_hi h_lo y_done y_copied")
        w_loaded = semaphores(nc, stack, "we_loaded_even we_loaded_odd")
        x_loaded = semaphores(nc, stack, " ".join(f"slot_loaded_{r}" for r in range(MOE_UNROLL)))
        y_stored = semaphores(nc, stack, " ".join(f"slot_stored_{r}" for r in range(MOE_UNROLL)))
        block = stack.enter_context(nc.Block())
        x_view = slots_dram.rearrange("(k p) c -> p k c", p=P)
        y_view = y_dram.rearrange("(k p) c -> p k c", p=P)
        ROUNDS = MOE_TILES // MOE_UNROLL
        TURN, GU, HT, DOWN = 1, 2, 3, 4

        def rounds(engine, body):
            body(0, lambda k: 0 <= k)
            body(1, lambda k: 0 <= k)
            with engine.Fori(2, ROUNDS) as it:
                body(it, lambda k: True)
            body(ROUNDS, lambda k: k < MOE_TILES)

        def tiles(it, valid):
            for r in range(MOE_UNROLL):
                k = MOE_UNROLL * it + r
                ok = (lambda back, k=k: valid(k - back) if isinstance(k, int) else True)
                yield k, r, ok

        @block.sync
        def _(sp):
            for e in range(E):
                wait(sp, w_lo_ready, e - 1)
                for w, at in ((a["Wg"], 0), (a["Wu"], I), (a["Wd"], 2 * I)):
                    sp.dma_start(w_raw[:, e % 2, :, at:at + I], w[e].rearrange("(c p) i -> p c i", p=P)).then_inc(w_loaded[e % 2], 16)

            def body(it, valid):
                for k, r, ok in tiles(it, valid):
                    if ok(0):
                        wait(sp, x_turned, k - 3)
                        sp.dma_start(x_in[:, r:r + 1], x_view[:, bass.ds(k, 1)]).then_inc(x_loaded[r], 16)
                    if ok(DOWN):
                        j, rj = k - DOWN, (r - DOWN) % MOE_UNROLL
                        wait(sp, y_copied, j + 1)
                        sp.dma_start(y_view[:, bass.ds(j, 1)], y_out[:, rj:rj + 1]).then_inc(y_stored[rj], 16)
            rounds(sp, body)
            for r in range(MOE_UNROLL):
                sp.wait_ge(y_stored[r], 16 * ROUNDS)

        @block.scalar
        def _(act):
            for e in range(E):
                act.wait_ge(w_loaded[e % 2], 48 * (e // 2 + 1))
                nc.scalar.activation(w_hi[:, e], w_raw[:, e % 2], ACT.Copy).then_inc(w_hi_ready, 1)

            def body(it, valid):
                for k, r, ok in tiles(it, valid):
                    if ok(TURN):
                        j, q = k - TURN, (r - TURN) % 2
                        act.wait_ge(x_turned, j + 1)
                        wait(act, gu_done, j - 1)
                        nc.scalar.activation(xt_hi[:, q], ps_xt[:, q, :C].rearrange("p (c t) -> p c t", c=KC),
                                             ACT.Copy).then_inc(x_hi, 1)
                    if ok(GU):
                        j, q = k - GU, (r - GU) % 2
                        act.wait_ge(gu_done, j + 1)
                        wait(act, clip_ready, j - 1)
                        nc.scalar.activation(gate[:, q], ps_gu[:, q, :I], ACT.Silu).then_inc(gate_ready, 1)
                    if ok(HT):
                        j, q = k - HT, (r - HT) % 2
                        act.wait_ge(h_turned, j + 1)
                        wait(act, y_done, j - 1)
                        nc.scalar.activation(ht_hi[:, q], ps_ht[:, q, :C].rearrange("p (c t) -> p c t", c=KC),
                                             ACT.Copy).then_inc(h_hi, 1)
                    if ok(DOWN):
                        j, q, rj = k - DOWN, (r - DOWN) % 2, (r - DOWN) % MOE_UNROLL
                        act.wait_ge(y_done, j + 1)
                        wait(act, y_stored[rj], 16 * (it - 1))
                        nc.scalar.activation(y_out[:, rj], ps_y[:, q, :C], ACT.Copy).then_inc(y_copied, 1)
            rounds(act, body)

        @block.gpsimd
        def _(pool):
            def body(it, valid):
                for k, r, ok in tiles(it, valid):
                    if ok(GU):
                        j, q = k - GU, (r - GU) % 2
                        pool.wait_ge(gate_ready, j + 1)
                        wait_alone(pool, inner_ready, j - 1, m["passed"])
                        nc.gpsimd.tensor_scalar(clipped[:, q], gate[:, q], LIMIT, -LIMIT, ALU.min, ALU.max).then_inc(clip_ready, 1)
            rounds(pool, body)

        @block.vector
        def _(dve):
            for e in range(E):
                dve.wait_ge(w_hi_ready, e + 1)
                nc.vector.tensor_tensor(w_lo[:, e], w_raw[:, e % 2], w_hi[:, e].bitcast(F32), ALU.subtract).then_inc(w_lo_ready, 1)

            def body(it, valid):
                for k, r, ok in tiles(it, valid):
                    if ok(TURN):
                        j, q = k - TURN, (r - TURN) % 2
                        dve.wait_ge(x_hi, j + 1)
                        nc.vector.tensor_tensor(xt_lo[:, q], ps_xt[:, q, :C].rearrange("p (c t) -> p c t", c=KC),
                                                xt_hi[:, q].bitcast(F32), ALU.subtract).then_inc(x_lo, 1)
                    if ok(HT):
                        j, q = k - HT, (r - HT) % 2
                        dve.wait_ge(h_hi, j + 1)
                        nc.vector.tensor_tensor(ht_lo[:, q], ps_ht[:, q, :C].rearrange("p (c t) -> p c t", c=KC),
                                                ht_hi[:, q].bitcast(F32), ALU.subtract).then_inc(h_lo, 1)
                    if ok(GU):
                        j, q = k - GU, (r - GU) % 2
                        dve.wait_ge(clip_ready, j + 1)
                        wait(dve, h_turned, j - 1)
                        nc.vector.tensor_tensor(inner[:, q], ps_gu[:, q, I:], clipped[:, q], ALU.mult).then_inc(inner_ready, 1)
            rounds(dve, body)

        @block.tensor
        def _(pe):
            pe.wait_ge(w_lo_ready, E)

            def body(it, valid):
                for k, r, ok in tiles(it, valid):
                    if ok(TURN):
                        j, q, rj = k - TURN, (r - TURN) % 2, (r - TURN) % MOE_UNROLL
                        pe.wait_ge(x_loaded[rj], 16 * (it + 1 - (r < TURN)))
                        wait(pe, x_lo, j - 1)
                        for c in range(KC):
                            last = nc.tensor.transpose(ps_xt[:, q, c * P:(c + 1) * P], x_in[:, rj, c * P:(c + 1) * P], m["ident"][:])
                        last.then_inc(x_turned, 1)
                    if ok(GU):
                        j, q = k - GU, (r - GU) % 2
                        e = pe.value_load(m["owner"][0:1, bass.ds(j, 1)], min_val=0, max_val=E - 1)
                        pe.wait_ge(x_lo, j + 1)
                        wait(pe, inner_ready, j - 1)
                        terms = [(w, v, c) for c in range(KC) for w, v in ((w_hi, xt_hi), (w_hi, xt_lo), (w_lo, xt_hi))]
                        for i, (w, v, c) in enumerate(terms):
                            last = nc.tensor.matmul(ps_gu[:, q], v[:, q, c], w[:, e, c, :2 * I], start=(i == 0), stop=(i == len(terms) - 1))
                        last.then_inc(gu_done, 1)
                    if ok(HT):
                        j, q = k - HT, (r - HT) % 2
                        pe.wait_ge(inner_ready, j + 1)
                        wait(pe, h_lo, j - 1)
                        for c in range(KC):
                            last = nc.tensor.transpose(ps_ht[:, q, c * P:(c + 1) * P], inner[:, q, c * P:(c + 1) * P], m["ident"][:])
                        last.then_inc(h_turned, 1)
                    if ok(DOWN):
                        j, q = k - DOWN, (r - DOWN) % 2
                        e = pe.value_load(m["owner"][0:1, bass.ds(j, 1)], min_val=0, max_val=E - 1)
                        pe.wait_ge(h_lo, j + 1)
                        wait(pe, y_copied, j - 1)
                        terms = [(w, v, c) for c in range(KC) for w, v in ((w_hi, ht_hi), (w_hi, ht_lo), (w_lo, ht_hi))]
                        for i, (w, v, c) in enumerate(terms):
                            last = nc.tensor.matmul(ps_y[:, q, :C], v[:, q, c], w[:, e, c, 2 * I:], start=(i == 0), stop=(i == len(terms) - 1))
                        last.then_inc(y_done, 1)
            rounds(pe, body)


def output_phase(nc, m, x, y_dram, out):
    with ExitStack() as stack:
        sb = lambda name, shape, dt=F32: stack.enter_context(nc.sbuf_tensor(name, shape, dt))
        ps = lambda name, shape: stack.enter_context(nc.psum_tensor(name, shape, F32))
        x_in, heads, both, biased, one_in, result = (sb(n, [P, 2, C]) for n in (
            "res_in", "heads", "both", "biased", "one_in", "result"))
        expert_y = sb("expert_y", [P, 2, 2, C])
        a_hi, a_lo = (sb(n, [P, 2, KC, P], F32R) for n in ("a_hi", "a_lo"))
        y_slot = sb("y_slot", [P, 2, 2, 1], U32)
        ps_at, ps_z = (ps(n, [P, 2, 512]) for n in ("ps_at", "ps_z"))
        (heads_ready, turned, hi_ready, lo_ready, projected, biased_ready, both_ready, one_ready, result_ready,
         slot_ready) = semaphores(nc, stack, "heads_ready heads_turned a_hi_ready a_lo_ready projected biased_ready "
                                  "both_ready one_ready result_ready slot_ready")
        x_loaded = semaphores(nc, stack, "res_loaded_even res_loaded_odd")
        gathered = semaphores(nc, stack, "gathered_even gathered_odd")
        stored = semaphores(nc, stack, "out_stored_even out_stored_odd")
        block = stack.enter_context(nc.Block())
        x_view = x.rearrange("b (j p) c -> p (b j) c", p=P)
        out_view = out.rearrange("b (j p) c -> p (b j) c", p=P)
        WO = 3 * C + E

        def rounds(engine, body):
            body(0)
            with engine.Fori(1, TILES // 2) as it:
                body(it)

        @block.sync
        def _(sp):
            def body(it):
                for r in range(2):
                    t = 2 * it + r
                    wait(sp, biased_ready, t - 1)
                    sp.dma_start(x_in[:, r:r + 1], x_view[:, bass.ds(t, 1)]).then_inc(x_loaded[r], 16)
                    if not isinstance(t, int) or t:
                        store(t - 1, 1 - r)

            def store(t, r):
                sp.wait_ge(result_ready, t + 1)
                sp.dma_start(out_view[:, bass.ds(t, 1)], result[:, r:r + 1]).then_inc(stored[r], 16)
            rounds(sp, body)
            store(TILES - 1, 1)
            for r in range(2):
                sp.wait_ge(stored[r], 16 * TILES // 2)

        @block.gpsimd
        def _(pool):
            def body(it):
                for r in range(2):
                    t = 2 * it + r
                    wait(pool, result_ready, t - 1)
                    nc.gpsimd.tensor_copy(y_slot[:, r], m["slot"][:, :, bass.ds(t, 1)]).then_inc(slot_ready, 1)
                    wait_alone(pool, slot_ready, t + 1, m["passed"])
                    for which in range(2):
                        nc.gpsimd.indirect_dma_start(
                            expert_y[:, r, which], None, y_dram,
                            bass.IndirectOffsetOnAxis(ap=y_slot[:, r, which], axis=0)).then_inc(gathered[r], 16)
            rounds(pool, body)

        @block.scalar
        def _(act):
            def body(it):
                for r in range(2):
                    t = 2 * it + r
                    wait(act, turned, t - 1)
                    nc.scalar.activation(heads[:, r].rearrange("p (g c) -> p g c", g=NG),
                                         m["attn"][:, :, t], ACT.Copy).then_inc(heads_ready, 1)
                    act.wait_ge(turned, t + 1)
                    wait(act, projected, t - 1)
                    nc.scalar.activation(a_hi[:, r], ps_at[:, r, :C].rearrange("p (c t) -> p c t", c=KC), ACT.Copy).then_inc(hi_ready, 1)
            rounds(act, body)

        @block.vector
        def _(dve):
            def body(it):
                for r in range(2):
                    t = 2 * it + r
                    dve.wait_ge(hi_ready, t + 1)
                    nc.vector.tensor_tensor(a_lo[:, r], ps_at[:, r, :C].rearrange("p (c t) -> p c t", c=KC),
                                            a_hi[:, r].bitcast(F32), ALU.subtract).then_inc(lo_ready, 1)
                    dve.wait_ge(x_loaded[r], 16 * (it + 1))
                    wait(dve, both_ready, t - 1)
                    nc.vector.tensor_tensor(biased[:, r], x_in[:, r], m["row_bias"][:, 1], ALU.add).then_inc(biased_ready, 1)
                    dve.wait_ge(biased_ready, t + 1)
                    dve.wait_ge(projected, t + 1)
                    wait(dve, one_ready, t - 1)
                    nc.vector.tensor_tensor(both[:, r], ps_z[:, r, :C], biased[:, r], ALU.add).then_inc(both_ready, 1)
                    dve.wait_ge(both_ready, t + 1)
                    dve.wait_ge(gathered[r], 32 * (it + 1))
                    wait(dve, result_ready, t - 1)
                    nc.vector.scalar_tensor_tensor(out=one_in[:, r], in0=expert_y[:, r, 0], scalar=m["weight"][:, 0, bass.ds(t, 1)],
                                                   in1=both[:, r], op0=ALU.mult, op1=ALU.add).then_inc(one_ready, 1)
                    dve.wait_ge(one_ready, t + 1)
                    wait(dve, stored[r], 16 * it)
                    nc.vector.scalar_tensor_tensor(out=result[:, r], in0=expert_y[:, r, 1], scalar=m["weight"][:, 1, bass.ds(t, 1)],
                                                   in1=one_in[:, r], op0=ALU.mult, op1=ALU.add).then_inc(result_ready, 1)
            rounds(dve, body)

        @block.tensor
        def _(pe):
            def body(it):
                for r in range(2):
                    t = 2 * it + r
                    pe.wait_ge(heads_ready, t + 1)
                    wait(pe, lo_ready, t - 1)
                    for c in range(KC):
                        last = nc.tensor.transpose(ps_at[:, r, c * P:(c + 1) * P], heads[:, r, c * P:(c + 1) * P], m["ident"][:])
                    last.then_inc(turned, 1)
                    pe.wait_ge(lo_ready, t + 1)
                    wait(pe, both_ready, t - 1)
                    terms = [(w, v, c) for c in range(KC) for w, v in ((m["w_hi"], a_hi), (m["w_hi"], a_lo), (m["w_lo"], a_hi))]
                    for i, (w, v, c) in enumerate(terms):
                        last = nc.tensor.matmul(ps_z[:, r, :C], v[:, r, c], w[:, c, WO:WO + C], start=(i == 0), stop=(i == len(terms) - 1))
                    last.then_inc(projected, 1)
            rounds(pe, body)


def program(nc, a, out):
    xn_dram = nc.dram_tensor("xn_scratch", (B * T, C), F32, kind="Internal").ap()
    parts_dram = nc.dram_tensor("parts_scratch", (3, 2, B, C, T), BF16, kind="Internal").ap()
    slots_dram = nc.dram_tensor("slots_scratch", (MOE_TILES * P, C), F32, kind="Internal").ap()
    y_dram = nc.dram_tensor("y_scratch", (MOE_TILES * P, C), F32, kind="Internal").ap()
    with ExitStack() as stack:
        shapes = {
            "w_hi": ([P, KC, 4 * C + E], F32R), "w_lo": ([P, KC, 4 * C + E], F32R),
            "qk_bias": ([P, 2, KC], F32), "row_bias": ([P, 2, C], F32), "eps": ([P, 1], F32),
            "ident": ([P, P], F32), "ident_b": ([P, P], BF16), "mask_b": ([P, P], BF16),
            "attn": ([P, NG, TILES, GC], F32), "logits": ([P, TILES, E], F32),
            "weight": ([P, 2, TILES], F32), "slot": ([P, 2, TILES], U32), "owner": ([P, MOE_TILES], U32),
        }
        m = {n: stack.enter_context(nc.sbuf_tensor(n, sh, dt)) for n, (sh, dt) in shapes.items()}
        m["passed"] = stack.enter_context(nc.semaphore("passed"))
        with ExitStack() as stack2:
            more = {"v_all": ([P, GROUPS, QT, GC], F32), "v_ext": ([P, 2, QT, HG, VW], F32)}
            m.update({n: stack2.enter_context(nc.sbuf_tensor(n, sh, dt)) for n, (sh, dt) in more.items()})
            setup_phase(nc, m, a)
            project_phase(nc, m, a["x"], xn_dram, parts_dram, slots_dram)
            route_phase(nc, m)
            with ExitStack() as stack3:
                more = {"q_stack": ([P, STACKS, HG, T], BF16), "k_stack": ([P, STACKS, HG, T], BF16)}
                m.update({n: stack3.enter_context(nc.sbuf_tensor(n, sh, dt)) for n, (sh, dt) in more.items()})
                attention_phase(nc, m, parts_dram, xn_dram, slots_dram)
        expert_phase(nc, m, a, slots_dram, y_dram)
        output_phase(nc, m, a["x"], y_dram, out)


NAMES = {"x": "L0_attn_idx", "Wq": "L0_attn_Wq", "bq": "L0_attn_bq", "Wk": "L0_attn_Wk", "bk": "L0_attn_bk",
         "Wv": "L0_attn_Wv", "bv": "L0_attn_bv", "Wo": "L0_attn_Wo", "bo": "L0_attn_bo", "Wr": "L0_ffn_Wr",
         "Wg": "L0_ffn_Wg", "Wu": "L0_ffn_Wu", "Wd": "L0_ffn_Wd"}


def kernel(**inputs):
    import concourse.bacc as bacc
    from concourse.bass_utils import run_bass_kernel_spmd

    nc = bacc.Bacc("TRN2", target_bir_lowering=False, num_devices=1)
    arrays, a = {}, {}
    for short, name in NAMES.items():
        v = np.ascontiguousarray(inputs[name])
        arrays[f"in_{short}"] = v
        a[short] = nc.dram_tensor(f"in_{short}", v.shape, mybir.dt.from_np(v.dtype), kind="ExternalInput").ap()
    out = nc.dram_tensor("out", (B, T, C), F32, kind="ExternalOutput").ap()
    program(nc, a, out)
    return run_bass_kernel_spmd(nc, [arrays], core_ids=[0]).results[0]["out"]
```

```python
from contextlib import ExitStack

import numpy as np
import concourse.bass as bass
from concourse import mybir

F32 = mybir.dt.float32
F32R = mybir.dt.float32r
BF16 = mybir.dt.bfloat16
U32 = mybir.dt.uint32
ACT = mybir.ActivationFunctionType
ALU = mybir.AluOpType
AX = mybir.AxisListType

P = 128
B, T, C = 4, 1024, 256
H, D = 16, 16
E, I = 8, 256
EPS = 1e-5
LIMIT = 7.0
MASKED = -1e30

KC = C // P
TILES = B * T // P
SUP = 4
SW = SUP * P
NSUP = TILES // SUP
HG = 4
NG = H // HG
GROUPS = B * NG
GC = HG * D
QT = T // P
SCALE = 1.0 / D ** 0.5
VW = 32

Q_PARTS = [0, 0, 0, 1, 1, 2]
K_PARTS = [0, 1, 2, 0, 1, 0]
PR = D * len(Q_PARTS)
SR = PR + 3
STACKS = NG


MOE_UNROLL = 8
MOE_TILES = -(-((2 * B * T + E * (P - 1)) // P) // MOE_UNROLL) * MOE_UNROLL
ZERO_TILES = MOE_TILES // NSUP
WE = 2 * I + C
RAW = 4
EARLY = 2
ROW = C + 1


def wait(engine, semaphore, value):
    if isinstance(value, int) and value <= 0:
        return
    engine.wait_ge(semaphore, value)


def wait_alone(engine, semaphore, value, passed):
    if isinstance(value, int) and value <= 0:
        return
    engine.wait_ge(semaphore, value)
    engine.sem_inc(passed, 1)


def semaphores(nc, stack, names):
    return [stack.enter_context(nc.semaphore(n)) for n in names.split()]


def load_expert(sp, a, e, w_raw, loaded):
    for w, at in ((a["Wg"], 0), (a["Wu"], I), (a["Wd"], 2 * I)):
        sp.dma_start(w_raw[:, :, at:at + I], w[e].rearrange("(c p) i -> p c i", p=P)).then_inc(loaded, 16)


def setup_phase(nc, m, a):
    with ExitStack() as stack:
        w_raw = stack.enter_context(nc.sbuf_tensor("w_raw", [P, KC, 4 * C + E], F32))
        loaded, built, hi_ready, lo_ready = semaphores(
            nc, stack, "weights_loaded constants_built weights_hi weights_lo")
        block = stack.enter_context(nc.Block())
        rows = lambda w: w.rearrange("(k p) c -> p k c", p=P)
        x_all = m["attn"][:].rearrange("p g t c -> p (g t c)").rearrange("p (n j c) -> p n j c", n=NSUP, j=SUP)
        x_view = a["x"].rearrange("b (n j p) c -> p (b n) j c", p=P, j=SUP)

        @block.sync
        def _(sp):
            for w, at in ((a["Wq"], 0), (a["Wk"], C), (a["Wv"], 2 * C), (a["Wr"], 3 * C), (a["Wo"], 3 * C + E)):
                sp.dma_start(w_raw[:, :, at:at + w.shape[1]], rows(w)).then_inc(loaded, 16)
            for n in range(2):
                sp.dma_start(x_all[:, n], x_view[:, n]).then_inc(m["x_loaded"][n], 16)
            for n, v in enumerate((a["bq"], a["bk"])):
                sp.dma_start(m["qk_bias"][:, n, :], v.rearrange("(k p) -> p k", p=P),
                             allow_slow_non_contiguous=True).then_inc(loaded, 16)
            for n, v in enumerate((a["bv"], a["bo"])):
                sp.dma_start(m["row_bias"][:, n, :], v.rearrange("(o c) -> o c", o=1).broadcast_to([P, C])).then_inc(loaded, 16)

        @block.scalar
        def _(act):
            act.wait_ge(loaded, 16 * 9)
            nc.scalar.activation(m["w_hi"][:], w_raw[:], ACT.Copy).then_inc(hi_ready, 1)
            act.wait_ge(lo_ready, 1)

        @block.vector
        def _(dve):
            nc.vector.memset(m["eps"][:], EPS)
            dve.wait_ge(hi_ready, 1)
            nc.vector.tensor_tensor(m["w_lo"][:], w_raw[:], m["w_hi"][:].bitcast(F32), ALU.subtract).then_inc(lo_ready, 1)

        @block.gpsimd
        def _(pool):
            zeros = nc.gpsimd.memset(m["ident"][:], 0.0)
            nc.gpsimd.memset(m["ident_b"][:], 0.0)
            nc.gpsimd.memset(m["mask_b"][:], 0.0).then_inc(built, 1)
            pool.wait_ge(built, 1)
            for t in (m["ident"], m["ident_b"]):
                nc.gpsimd.affine_select(out=t[:], in_=t[:], compare_op=ALU.not_equal, fill=1.0, base=0,
                                        pattern=[[-1, P]], channel_multiplier=1)
            nc.gpsimd.affine_select(out=m["mask_b"][:], in_=m["mask_b"][:], compare_op=ALU.is_ge, fill=MASKED,
                                    base=0, pattern=[[-1, P]], channel_multiplier=1)
            for par in range(2):
                nc.gpsimd.memset(m["v_ext"][:, par], 0.0).then_inc(built, 1)
            pool.wait_ge(built, 3)
            for par in range(2):
                nc.gpsimd.memset(m["v_ext"][:, par, :, :, D:D + 1], 1.0).then_inc(built, 1)


def project_phase(nc, m, x, xn_dram, parts_dram, slots_dram):
    with ExitStack() as stack:
        sb = lambda name, shape, dt=F32: stack.enter_context(nc.sbuf_tensor(name, shape, dt))
        ps = lambda name, shape: stack.enter_context(nc.psum_tensor(name, shape, F32))
        x_all = m["attn"][:].rearrange("p g t c -> p (g t c)").rearrange("p (n j c) -> p n j c", n=NSUP, j=SUP)
        xn = sb("xn", [P, 2, SUP, C])
        xt_hi, xt_lo = sb("xt_hi", [P, 2, KC, SW], F32R), sb("xt_lo", [P, 2, KC, SW], F32R)
        part, rest = sb("part", [P, 2, 3, 2, KC, SW], BF16), sb("rest", [P, 2, 2, KC, SW])
        stats, mv = sb("stats", [P, SUP, 6]), sb("mv", [P, 2, SUP, 2])
        std, rstd = sb("std", [P, 2, SUP]), sb("rstd", [P, 2, SUP])
        ps_xt, ps_qk, ps_v = ps("ps_xt", [P, KC, SW]), ps("ps_qk", [P, 2, KC, SW]), ps("ps_v", [P, 2, 512])
        (stats_ready, mv_ready, std_ready, rstd_ready, xn_ready, xt_in_psum, hi_ready, lo_ready, qk_in_psum,
         part0_ready, rest_ready, part1_ready, part2_ready, v_in_psum, v_ready) = semaphores(
            nc, stack, "stats_ready mv_ready std_ready rstd_ready xn_ready xt_in_psum hi_ready lo_ready qk_in_psum "
            "part0_ready rest_ready part1_ready part2_ready v_in_psum v_ready")
        zeros = m["we_raw"][:].rearrange("p e c w -> p (e c w)")[:, :ZERO_TILES * ROW].rearrange("p (t c) -> p t c", c=ROW)
        spare = sb("spare", [P, MOE_TILES], U32)
        zeros_ready, zeroed, spare_ready = semaphores(nc, stack, "zeros_ready zeroed spare_ready")
        x_loaded = m["x_loaded"]
        xn_stored = semaphores(nc, stack, "xn_stored_even xn_stored_odd")
        stored = semaphores(nc, stack, "parts_stored_even parts_stored_odd")
        block = stack.enter_context(nc.Block())
        x_view = x.rearrange("b (n j p) c -> p (b n) j c", p=P, j=SUP)
        xn_view = xn_dram.rearrange("(n j p) c -> p n j c", p=P, j=SUP)
        parts_view = parts_dram.rearrange("r a b (k p) (h t) -> r a k h p b t", p=P, t=SW)
        units = [(q, k) for q in range(2) for k in range(KC)]
        PARTS_STORED = 16 * 3 * len(units)

        def rounds(engine, body):
            body(0, False)
            with engine.Fori(1, NSUP // 2 - 1) as it:
                body(it, False)
            body(NSUP // 2 - 1, True)

        @block.sync
        def _(sp):
            for n in range(2, NSUP):
                wait(sp, x_loaded[n % 2], 16 * (n // 2))
                sp.dma_start(x_all[:, n], x_view[:, n]).then_inc(x_loaded[n % 2], 16)

            def body(it, last):
                for par in range(2):
                    n = 2 * it + par
                    wait(sp, part2_ready, 4 * (n + 1))
                    for r in range(3):
                        for q, k in units:
                            sp.dma_start(parts_view[r, q, k, par][:, bass.ds(it, 1)],
                                         part[:, par, r, q, k].rearrange("p (o t) -> p o t", o=1)).then_inc(stored[par], 16)
            rounds(sp, body)
            for par in range(2):
                sp.wait_ge(xn_stored[par], 16 * NSUP // 2)
                sp.wait_ge(stored[par], PARTS_STORED * NSUP // 2)

        def root(n, par):
            nc.scalar.wait_ge(mv_ready, n + 1)
            nc.scalar.activation(std[:, par], mv[:, par, :, 1], ACT.Sqrt, bias=m["eps"][:, 0:1]).then_inc(std_ready, 1)

        @block.scalar
        def _(act):
            def hi(n, par):
                act.wait_ge(xt_in_psum, n + 1)
                wait(act, v_in_psum, SUP * (n - 1))
                nc.scalar.activation(xt_hi[:, par], ps_xt[:], ACT.Copy).then_inc(hi_ready, 1)
                act.dma_start(xn_view[:, bass.ds(n, 1)], xn[:, par:par + 1]).then_inc(xn_stored[par], 16)

            def body(it, last):
                for par in range(2):
                    n = 2 * it + par
                    if not last:
                        root(n + 2, par)
                    if not (last and par):
                        hi(n + 1, 1 - par)
                    for u, (q, k) in enumerate(units):
                        act.wait_ge(qk_in_psum, 4 * n + u + 1)
                        wait(act, stored[par], PARTS_STORED * it)
                        nc.scalar.activation(part[:, par, 0, q, k], ps_qk[:, q, k], ACT.Identity,
                                             bias=m["qk_bias"][:, q, k:k + 1]).then_inc(part0_ready, 1)
                        if u:
                            second_part(n, par, u - 1)
                    second_part(n, par, len(units) - 1)

            def second_part(n, par, u):
                q, k = units[u]
                act.wait_ge(rest_ready, 4 * n + u + 1)
                nc.scalar.activation(part[:, par, 1, q, k], rest[:, par, q, k], ACT.Copy).then_inc(part1_ready, 1)
            root(0, 0)
            root(1, 1)
            hi(0, 0)
            rounds(act, body)

        @block.vector
        def _(dve):
            def moments(n, par, it):
                dve.wait_ge(x_loaded[par], 16 * (it + 1))
                wait(dve, mv_ready, n)
                for j in range(SUP):
                    last = nc.vector.bn_stats(stats[:, j], x_all[:, n, j])
                last.then_inc(stats_ready, 1)
                wait_alone(dve, stats_ready, n + 1, m["passed"])
                for j in range(SUP):
                    last = nc.vector.bn_aggr(mv[:, par, j], stats[:, j])
                last.then_inc(mv_ready, 1)

            def normalise(n, par, it):
                dve.wait_ge(std_ready, n + 1)
                nc.vector.reciprocal(rstd[:, par], std[:, par]).then_inc(rstd_ready, 1)
                dve.wait_ge(rstd_ready, n + 1)
                wait(dve, xt_in_psum, n - 1)
                wait(dve, xn_stored[par], 16 * it)
                for j in range(SUP):
                    last = nc.vector.tensor_scalar(xn[:, par, j],
                                                   x_all[:, n, j],
                                                   mv[:, par, j, 0:1], rstd[:, par, j:j + 1], ALU.subtract, ALU.mult)
                last.then_inc(xn_ready, 1)

            def lo(n, par):
                dve.wait_ge(hi_ready, n + 1)
                nc.vector.tensor_tensor(xt_lo[:, par], ps_xt[:], xt_hi[:, par].bitcast(F32), ALU.subtract).then_inc(lo_ready, 1)

            def body(it, last):
                for par in range(2):
                    n = 2 * it + par
                    if not last:
                        moments(n + 2, par, it + 1)
                    if not (last and par):
                        lo(n + 1, 1 - par)
                    if not last:
                        normalise(n + 2, par, it + 1)
                    for u, (q, k) in enumerate(units):
                        dve.wait_ge(part0_ready, 4 * n + u + 1)
                        wait(dve, part2_ready, 4 * (n - 1))
                        nc.vector.scalar_tensor_tensor(out=rest[:, par, q, k], in0=ps_qk[:, q, k],
                                                       scalar=m["qk_bias"][:, q, k:k + 1], in1=part[:, par, 0, q, k],
                                                       op0=ALU.add, op1=ALU.subtract).then_inc(rest_ready, 1)
                    for j in range(SUP):
                        dve.wait_ge(v_in_psum, SUP * n + j + 1)
                        nc.vector.tensor_tensor(
                            m["v_all"][:, bass.ds(NG * it, NG), SUP * par + j, :],
                            ps_v[:, j % 2, :C].rearrange("p (g c) -> p g c", g=NG),
                            m["row_bias"][:, 0].rearrange("p (g c) -> p g c", g=NG), ALU.add)
                        nc.vector.tensor_copy(m["logits"][:, SUP * n + j],
                                              ps_v[:, j % 2, C:C + E]).then_inc(v_ready, 1)
            for n in range(2):
                moments(n, n, 0)
            for n in range(2):
                normalise(n, n, 0)
            lo(0, 0)
            rounds(dve, body)

        @block.gpsimd
        def _(pool):
            nc.gpsimd.memset(m["k_stack"][PR:P], 1.0).then_inc(zeros_ready, 1)
            pool.wait_ge(zeros_ready, 1)
            nc.gpsimd.memset(zeros, 0.0).then_inc(zeros_ready, 1)
            nc.gpsimd.iota(m["token_row"][:], [[2 * P, TILES], [1, 2]], base=0, channel_multiplier=2)
            pool.wait_ge(zeros_ready, 2)
            nc.gpsimd.iota(spare[:], [[P, MOE_TILES]], base=2 * B * T, channel_multiplier=1).then_inc(zeros_ready, 1)
            pool.wait_ge(zeros_ready, 3)

            def body(it, last):
                for par in range(2):
                    n = 2 * it + par
                    wait_alone(pool, zeroed, 16 * n, m["passed"])
                    nc.gpsimd.tensor_copy(zeros[:, :, C:].bitcast(U32),
                                          spare[:, bass.ds(ZERO_TILES * n, ZERO_TILES)].rearrange("p (j o) -> p j o", o=1)).then_inc(spare_ready, 1)
                    wait_alone(pool, xn_ready, n + 1, m["passed"])
                    wait_alone(pool, spare_ready, n + 1, m["passed"])
                    pool.dma_start(slots_dram.rearrange("(i j p) c -> p i j c", p=P, j=ZERO_TILES)[:, bass.ds(n, 1)],
                                   zeros[:].rearrange("p (o j) c -> p o j c", o=1)).then_inc(zeroed, 16)
                    wait(pool, stored[par], PARTS_STORED * it)
                    for u, (q, k) in enumerate(units):
                        wait_alone(pool, part1_ready, 4 * n + u + 1, m["passed"])
                        nc.gpsimd.tensor_tensor(part[:, par, 2, q, k], rest[:, par, q, k], part[:, par, 1, q, k],
                                                ALU.subtract).then_inc(part2_ready, 1)
            rounds(pool, body)
            pool.wait_ge(zeroed, 16 * NSUP)

        @block.tensor
        def _(pe):
            passes = lambda par: ((m["w_hi"], xt_hi), (m["w_hi"], xt_lo), (m["w_lo"], xt_hi))

            def transposes(n, par):
                pe.wait_ge(xn_ready, n + 1)
                wait(pe, lo_ready, n)
                for j in range(SUP):
                    for k in range(KC):
                        last = nc.tensor.transpose(
                            ps_xt[:, k, j * P:(j + 1) * P],
                            xn[:, par, j, k * P:(k + 1) * P], m["ident"][:])
                last.then_inc(xt_in_psum, 1)

            def body(it, last):
                for par in range(2):
                    n = 2 * it + par
                    if not (last and par):
                        transposes(n + 1, 1 - par)
                    pe.wait_ge(lo_ready, n + 1)
                    for u, (q, k) in enumerate(units):
                        wait(pe, rest_ready, 4 * n + u - 3)
                        terms = [(w, v, c) for c in range(KC) for w, v in passes(par)]
                        for i, (w, v, c) in enumerate(terms):
                            last_mm = nc.tensor.matmul(ps_qk[:, q, k], w[:, c, q * C + k * P:q * C + (k + 1) * P],
                                                       v[:, par, c], start=(i == 0), stop=(i == len(terms) - 1))
                        last_mm.then_inc(qk_in_psum, 1)
                    for j in range(SUP):
                        wait(pe, v_ready, SUP * n + j - 1)
                        for i, (w, v, c) in enumerate(terms):
                            last_mm = nc.tensor.matmul(ps_v[:, j % 2, :C + E], v[:, par, c, j * P:(j + 1) * P],
                                                       w[:, c, 2 * C:3 * C + E], start=(i == 0), stop=(i == len(terms) - 1))
                        last_mm.then_inc(v_in_psum, 1)
            transposes(0, 0)
            rounds(pe, body)




def route_phase(nc, m):
    with ExitStack() as stack:
        sb = lambda name, shape, dt=F32: stack.enter_context(nc.sbuf_tensor(name, shape, dt))
        ps = lambda name, shape: stack.enter_context(nc.psum_tensor(name, shape, F32))
        cell = [P, TILES, E]
        order, left, first, second, t0 = (sb(n, cell) for n in ("order", "left", "first", "second", "t0"))
        top1, top2, pick, gap, total = (sb(n, [P, TILES]) for n in ("top1", "top2", "pick", "gap", "total"))
        chosen, upper, ones = sb("chosen", cell, BF16), sb("upper", [P, P], BF16), sb("ones", [P, P], BF16)
        scan = sb("scan", [P, 2, TILES, E])
        need, need_int, start = sb("need", [P, E]), sb("need_int", [P, E], mybir.dt.int32), sb("start", [P, 4, E])
        number, owner = sb("number", [P, MOE_TILES, E]), sb("owners", [P, MOE_TILES])
        ps_rank, ps_count = ps("ps_rank", cell), ps("ps_count", cell)
        step, built, made, exp_ready, gap_ready, chosen_ready, counted = semaphores(
            nc, stack, "route_step built made exp_ready gap_ready chosen_ready counted")
        block = stack.enter_context(nc.Block())
        per_tile = lambda v: v.rearrange("p (t o) -> p t o", o=1).broadcast_to(cell)
        per_expert = lambda v, n: v.rearrange("p (o e) -> p o e", o=1).broadcast_to([P, n, E])

        @block.gpsimd
        def _(pool):
            nc.gpsimd.iota(order[:], [[0, TILES], [-1, E]], base=E, channel_multiplier=0,
                           allow_small_or_imprecise_dtypes=True).then_inc(built, 1)
            nc.gpsimd.iota(number[:], [[1, MOE_TILES], [0, E]], base=0, channel_multiplier=0,
                           allow_small_or_imprecise_dtypes=True).then_inc(built, 1)
            nc.gpsimd.memset(ones[:], 1.0).then_inc(built, 1)
            pool.wait_ge(built, 3)
            nc.gpsimd.affine_select(out=upper[:], in_=ones[:], compare_op=ALU.is_gt, fill=0.0, base=0,
                                    pattern=[[1, P]], channel_multiplier=-1).then_inc(built, 1)

        @block.scalar
        def _(act):
            act.wait_ge(gap_ready, 1)
            nc.scalar.activation(gap[:], gap[:], ACT.Exp).then_inc(exp_ready, 1)

        @block.tensor
        def _(pe):
            pe.wait_ge(built, 4)
            pe.wait_ge(chosen_ready, 1)
            nc.tensor.matmul(ps_rank[:], upper[:], chosen[:], start=True, stop=True)
            nc.tensor.matmul(ps_count[:], ones[:], chosen[:], start=True, stop=True).then_inc(counted, 1)

        @block.vector
        def _(dve):
            chain = [0]

            def link(ins):
                chain[0] += 1
                ins.then_inc(step, 1)
                dve.wait_ge(step, chain[0])
            tt, ts = nc.vector.tensor_tensor, nc.vector.tensor_scalar
            logits = m["logits"][:]

            def best(scores, top, mark):
                link(nc.vector.tensor_reduce(top[:], scores, AX.X, ALU.max))
                link(tt(t0[:], scores, per_tile(top[:]), ALU.is_equal))
                link(tt(t0[:], t0[:], order[:], ALU.mult))
                link(nc.vector.tensor_reduce(pick[:], t0[:], AX.X, ALU.max))
                link(tt(mark[:], t0[:], per_tile(pick[:]), ALU.is_equal))
            dve.wait_ge(built, 4)
            best(logits, top1, first)
            link(ts(left[:], first[:], MASKED, None, ALU.mult))
            link(tt(left[:], left[:], logits, ALU.add))
            best(left[:], top2, second)
            tt(chosen[:], first[:], second[:], ALU.add).then_inc(chosen_ready, 1)
            tt(gap[:], top2[:], top1[:], ALU.subtract).then_inc(gap_ready, 1)
            dve.wait_ge(exp_ready, 1)
            link(ts(total[:], gap[:], 1.0, None, ALU.add))
            link(nc.vector.reciprocal(m["weight"][:, 0], total[:]))
            link(tt(m["weight"][:, 1], gap[:], m["weight"][:, 0], ALU.mult))

            dve.wait_ge(counted, 1)
            link(nc.vector.tensor_copy(scan[:, 0], ps_count[:]))
            at, shift = 0, 1
            while shift < TILES:
                nc.vector.tensor_copy(scan[:, 1 - at, :shift], scan[:, at, :shift])
                link(tt(scan[:, 1 - at, shift:], scan[:, at, shift:], scan[:, at, :TILES - shift], ALU.add))
                at, shift = 1 - at, 2 * shift
            incl = scan[:, at]
            link(ts(need[:], incl[:, TILES - 1], 1.0 / P, (P - 1.0) / P - 0.498, ALU.mult, ALU.add))
            link(nc.vector.tensor_copy(need_int[:], need[:]))
            link(nc.vector.tensor_copy(need[:], need_int[:]))
            link(nc.vector.memset(start[:, 0], 0.0))
            link(nc.vector.tensor_copy(start[:, 0, 1:], need[:, :E - 1]))
            for n, shift in enumerate((1, 2, 4)):
                nc.vector.tensor_copy(start[:, n + 1, :shift], start[:, n, :shift])
                link(tt(start[:, n + 1, shift:], start[:, n, shift:], start[:, n, :E - shift], ALU.add))
            link(tt(t0[:], incl, ps_count[:], ALU.subtract))
            link(tt(t0[:], t0[:], ps_rank[:], ALU.add))
            link(ts(need[:], start[:, 3], float(P), None, ALU.mult))
            link(tt(t0[:], t0[:], per_expert(need[:], TILES), ALU.add))
            for n, mark in enumerate((first, second)):
                link(tt(left[:], t0[:], mark[:], ALU.mult))
                link(nc.vector.tensor_reduce(total[:], left[:], AX.X, ALU.add))
                link(nc.vector.tensor_copy(m["slot"][:, n], total[:]))
            link(tt(number[:], per_expert(start[:, 3], MOE_TILES), number[:], ALU.is_le))
            link(nc.vector.tensor_reduce(owner[:], number[:, :, 1:], AX.X, ALU.add))
            link(nc.vector.tensor_copy(m["owner"][:], owner[:]))


STEPS = [(half, i) for half in range(2) for i in [0, *range(max(4 * half, 1), 4 * half + 4), *range(1, 4 * half)]]
DIAGONAL = [s for s, (half, i) in enumerate(STEPS) if i >= 4 * half]
LAG = 2
P_SETS = 3
S_BANKS = 3
MAX_UNITS = [(j, h, n) for j in range(QT) for n in (4 if j < 2 else 2 if j < 4 else 1,) for h in range(0, HG, n)]
AHEAD = 4
ROWS_BEHIND = 16
RING = ([("max", 1, u) for u in range(AHEAD, ROWS_BEHIND)] + [("rows", 0, 0)]
        + [("max", 1, u) for u in range(ROWS_BEHIND, len(MAX_UNITS))] + [("turn", 1, 0)]
        + [("max", 2, u) for u in range(AHEAD)] + [("rows", 0, 1)])
def ring_places():
    def columns(r):
        if r[0] == "rows":
            return SW
        j, _, heads = MAX_UNITS[r[2]]
        return (j + 1) * P * heads + P

    step_width = [SW * (half + 1) - max(SW * half, P * i) + P for half, i in STEPS]
    head_places = [(s, h) for s in range(len(STEPS)) for h in range(HG)]
    units = RING[:RING.index(("turn", 1, 0))]
    total, all_time = sum(map(columns, units)), HG * sum(step_width)
    places, at, time = {}, 0, 0
    for n, r in enumerate(units):
        while at < len(head_places) - 1 and time * total < sum(map(columns, units[:n])) * all_time:
            time += step_width[head_places[at][0]]
            at += 1
        places[r] = head_places[at]
    return places


RING_PLACE = {r: "end" for r in RING}
RING_PLACE.update(ring_places())
RING_PLACE["turn", 1, 0] = (len(STEPS), "sums")
FIRST_RING = [("max", 0, u) for u in range(len(MAX_UNITS))] + [("turn", 0, 0)] + [("max", 1, u) for u in range(AHEAD)]


def attention_phase(nc, m, a, parts_dram, xn_dram, slots_dram):
    with ExitStack() as stack:
        sb = lambda name, shape, dt=F32: stack.enter_context(nc.sbuf_tensor(name, shape, dt))
        ps = lambda name, shape: stack.enter_context(nc.psum_tensor(name, shape, F32))
        prob, heads_out = sb("prob", [P, P_SETS, HG, SW]), sb("heads_out", [P, 2, SW])
        neg_max, max_part = sb("neg_max", [P, 2, HG, QT]), sb("max_part", [HG * QT, 2, 3, P], BF16)
        max_rest, recip = sb("max_rest", [HG * QT, P]), sb("recip", [P, 2, 4, HG])
        ps_ring, ps_s, ps_o = ps("ps_ring", [P, 2, 1024]), ps("ps_s", [P, S_BANKS, SW]), ps("ps_o", [P, SW])
        (scores_done, exp_done, masked, values_done, ring_done, ring_free, split, split_ready, copied, recip_ready,
         v_ready) = semaphores(nc, stack, "scores_done exp_done masked values_done ring_done ring_free "
                               "split split_ready heads_copied recip_ready v_ext_ready")
        loaded = semaphores(nc, stack, "stack_loaded_even stack_loaded_odd")
        max_loaded = semaphores(nc, stack, "max_loaded_even max_loaded_odd")
        rows, row_slot = sb("rows", [P, 2, 2, 2, ROW]), sb("row_slot", [P, 2, 2, 2], U32)
        rows_loaded = semaphores(nc, stack, "rows_loaded_even rows_loaded_odd")
        scattered = semaphores(nc, stack, "scattered_even scattered_odd")
        slot_copied, rows_free = semaphores(nc, stack, "slot_copied rows_free")
        rows_view = xn_dram.rearrange("(n j p) c -> p n j c", p=P, j=2)
        block = stack.enter_context(nc.Block())
        q_stack, k_stack, v_ext, attn = m["q_stack"], m["k_stack"], m["v_ext"], m["attn"]
        view = parts_dram.rearrange("r a b (g h d) t -> a r (b g) d h t", g=NG, d=D)
        LOADS = 16 * 2 * len(Q_PARTS)
        NS = len(STEPS)

        def rounds(engine, body):
            with engine.Fori(0, B - 1) as it:
                for g in range(NG):
                    body(NG * it + g, it, g, False)
            for g in range(NG):
                body(NG * (B - 1) + g, B - 1, g, True)

        def group_pairs(it, g):
            return NG // 2 * it + g // 2

        def ring_units(it, g, last):
            before = len(FIRST_RING) + len(RING) * (NG * it + g)
            units = RING
            if last:
                units = [r for r in RING if g + r[1] < NG]
                before -= sum(q + r[1] >= NG for q in range(g) for r in RING)
            start = (len(FIRST_RING) + len(RING) * g - (sum(q + r[1] >= NG for q in range(g) for r in RING) if last else 0)) % 2
            return [(r, before + v, (start + v) % 2) for v, r in enumerate(units)]

        def score_bank(s, h):
            return (HG * s + h) % S_BANKS

        def width(s):
            half, i = STEPS[s]
            first = max(SW * half, P * i)
            return first, SW * (half + 1) - first

        @block.sync
        def _(sp):
            def load(n, g, buf):
                for which, (stk, parts) in enumerate(((q_stack, Q_PARTS), (k_stack, K_PARTS))):
                    for r, part in enumerate(parts):
                        sp.dma_start(stk[D * r:D * (r + 1), buf], view[which, part, n]).then_inc(loaded[g % 2], 16)

            def max_rows(k2, g):
                sp.wait_ge(split_ready, k2)
                for r in range(3):
                    sp.dma_start(q_stack[PR + r:PR + r + 1, g % STACKS].rearrange("o h (j t) -> o (h j) t", t=P),
                                 max_part[:, g % 2, r]).then_inc(max_loaded[g % 2], 16)
            def load_rows(n, it, g):
                wait_alone(sp, rows_free, n + 1, m["passed"])
                for which in range(2):
                    sp.dma_start(rows[:, g % 2:g % 2 + 1, :, which, :C], rows_view[:, bass.ds(n, 1)]).then_inc(rows_loaded[g % 2], 16)
            for n in range(2):
                load(n, n, n)
            load_rows(0, 0, 0)
            max_rows(1, 0)

            def body(n, it, g, last):
                if last and g + 1 == NG:
                    for e in range(EARLY):
                        load_expert(sp, a, e, m["we_raw"][:, e], m["we_loaded"][e])
                if not (last and g + 2 >= NG):
                    sp.wait_ge(scores_done, len(STEPS) * HG * n + 1)
                    load(n + 2, g, (g + 2) % STACKS)
                if not (last and g + 1 >= NG):
                    load_rows(n + 1, it, g + 1)
                    max_rows(n + 2, g + 1)
            rounds(sp, body)

        @block.gpsimd
        def _(pool):
            def values(n, g):
                nc.gpsimd.tensor_copy(v_ext[:, g % 2, :, :, :D],
                                      m["v_all"][:, n].rearrange("p k (h d) -> p k h d", h=HG)).then_inc(v_ready, 1)
            values(0, 0)
            pool.sem_inc(rows_free, 2)

            def scatter(n, it, g):
                nc.gpsimd.tensor_copy(row_slot[:, g % 2], m["slot"][:, :, bass.ds(2 * n, 2)]).then_inc(slot_copied, 1)
                nc.gpsimd.tensor_copy(rows[:, g % 2, :, :, C:].bitcast(U32).rearrange("p j w o -> p j (w o)"),
                                      m["token_row"][:, bass.ds(2 * n, 2), :]).then_inc(slot_copied, 1)
                pool.wait_ge(slot_copied, 2 * n + 2)
                wait_alone(pool, rows_loaded[g % 2], 32 * (group_pairs(it, g) + 1), m["passed"])
                for j in range(2):
                    for which in range(2):
                        nc.gpsimd.indirect_dma_start(
                            slots_dram, bass.IndirectOffsetOnAxis(ap=row_slot[:, g % 2, which, j:j + 1], axis=0),
                            rows[:, g % 2, j, which], None).then_inc(scattered[g % 2], 16)

            def body(n, it, g, last):
                for d, s in enumerate(DIAGONAL):
                    wait_alone(pool, exp_done, S_BANKS + HG * (NS * n + s + 1), m["passed"])
                    block_ = prob[:, s % P_SETS, :, :P]
                    nc.gpsimd.affine_select(out=block_, in_=block_, compare_op=ALU.is_ge, fill=0.0, base=0,
                                            pattern=[[0, HG], [1, P]], channel_multiplier=-1).then_inc(masked, 1)
                    if d == 1 and not (last and g + 1 >= NG):
                        pool.wait_ge(values_done, P_SETS + NS * n)
                        values(n + 1, g + 1)
                    if d == 2:
                        scatter(n, it, g)
                wait_alone(pool, scattered[g % 2], 64 * (group_pairs(it, g) + 1), m["passed"])
                pool.sem_inc(rows_free, 1)
            rounds(pool, body)

        @block.scalar
        def _(act):
            act.sem_inc(exp_done, S_BANKS)
            act.sem_inc(copied, 1)

            def copy_out(n, g, half, at):
                act.wait_ge(values_done, P_SETS + NS * n + (4, NS)[half])
                act.wait_ge(ring_done, at - len(RING))
                nc.scalar.activation(heads_out[:, half], ps_o[:], ACT.Copy).then_inc(copied, 1)

            def body(n, it, g, last):
                for s in range(NS):
                    for h in range(HG):
                        _, w = width(s)
                        U = HG * (NS * n + s) + h
                        act.wait_ge(scores_done, U + 1)
                        if h == 0:
                            act.wait_ge(values_done, NS * n + s + 1)
                        nc.scalar.activation(prob[:, s % P_SETS, h, :w], ps_s[:, score_bank(s, h), :w], ACT.Exp,
                                             scale=SCALE).then_inc(exp_done, 1)
                        if (s, h) == (6, 0):
                            copy_out(n, g, 0, len(FIRST_RING) + len(RING) * n)
                copy_out(n, g, 1, len(FIRST_RING) + len(RING) * n)
            rounds(act, body)

        @block.vector
        def _(dve):
            def ring(unit, n, it, g, at, slot):
                kind, ahead, u = unit
                dve.wait_ge(ring_done, at + 1)
                gg = g + ahead
                if kind == "max":
                    j, h, heads = MAX_UNITS[u]
                    w = (j + 1) * P
                    stride = 1024 // heads if j else P
                    if heads == 2:
                        stride = 512
                    src = ps_ring[:, slot, :heads * stride].rearrange("p (h w) -> p h w", h=heads)[:, :, :w]
                    nc.vector.tensor_reduce(neg_max[:, gg % 2, h:h + heads, j], src, AX.X, ALU.max,
                                            negate=True).then_inc(ring_free, 1)
                elif kind == "turn":
                    src = ps_ring[:HG * QT, slot, :P]
                    mp, rest = max_part[:, gg % 2], max_rest[:]
                    before = 4 * (n + ahead)
                    nc.vector.tensor_copy(mp[:, 0], src).then_inc(split, 1)
                    dve.wait_ge(split, before + 1)
                    nc.vector.tensor_tensor(rest, src, mp[:, 0], ALU.subtract).then_inc(split, 1)
                    dve.wait_ge(split, before + 2)
                    nc.vector.tensor_copy(mp[:, 1], rest).then_inc(split, 1)
                    dve.wait_ge(split, before + 3)
                    nc.vector.tensor_tensor(mp[:, 2], rest, mp[:, 1], ALU.subtract).then_inc(split, 1)
                    dve.wait_ge(split, before + 4)
                    dve.sem_inc(split_ready, 1)
                    dve.sem_inc(ring_free, 1)
                else:
                    src = ps_ring[:, slot, :SW].rearrange("p (j h v) -> p j h v", j=4, h=HG)
                    rc = recip[:, u]
                    nc.vector.reciprocal(rc, src[:, :, :, D]).then_inc(recip_ready, 1)
                    dve.wait_ge(recip_ready, 2 * n + u + 1)
                    dst = attn[:, g, bass.ds(QT * it + 4 * u, 4)].rearrange("p j (h d) -> p j h d", h=HG)
                    nc.vector.tensor_tensor(dst, src[:, :, :, :D], rc.rearrange("p j (h o) -> p j h o", o=1).broadcast_to([P, 4, HG, D]),
                                            ALU.mult).then_inc(ring_free, 1)

            for v, r in enumerate(FIRST_RING):
                ring(r, 0, 0, 0, v, v % 2)

            def body(n, it, g, last):
                for r, at, slot in ring_units(it, g, last):
                    ring(r, n, it, g, at, slot)
            rounds(dve, body)

        @block.tensor
        def _(pe):
            def ring(unit, n, it, g, at, slot):
                kind, ahead, u = unit
                gg = g + ahead
                if kind == "turn":
                    wait(pe, ring_free, at)
                    nc.tensor.transpose(ps_ring[:HG * QT, slot, :P], neg_max[:, gg % 2].rearrange("p h j -> p (h j)"),
                                        m["ident"][:]).then_inc(ring_done, 1)
                    return
                wait(pe, ring_free, at - 1)
                if kind == "rows":
                    pe.wait_ge(copied, 2 * n + u + 2)
                    for j in range(4):
                        last = nc.tensor.transpose(ps_ring[:, slot, P * j:P * (j + 1)],
                                                   heads_out[:, u, P * j:P * (j + 1)], m["ident"][:])
                    last.then_inc(ring_done, 1)
                    return
                j, h0, heads = MAX_UNITS[u]
                if u == 0:
                    pe.wait_ge(loaded[gg % 2], LOADS * (group_pairs(it, gg) + 1))
                buf = gg % STACKS
                stride = P if heads == 4 and j == 0 else 256 if heads == 4 else 512
                for hh in range(heads):
                    q = q_stack[:PR, buf, h0 + hh, P * j:P * (j + 1)]
                    w = (j + 1) * P
                    for c in range(0, w, SW):
                        cw = min(SW, w - c)
                        at_ = hh * stride + c
                        diagonal = c + cw == w
                        nc.tensor.matmul(ps_ring[:, slot, at_:at_ + cw], q, k_stack[:PR, buf, h0 + hh, c:c + cw],
                                         start=True, stop=not diagonal)
                    at_ = hh * stride + w - P
                    last = nc.tensor.matmul(ps_ring[:, slot, at_:at_ + P], m["ident_b"][:], m["mask_b"][:],
                                            start=False, stop=True)
                last.then_inc(ring_done, 1)

            for v, r in enumerate(FIRST_RING):
                ring(r, 0, 0, 0, v, v % 2)
            pe.sem_inc(values_done, P_SETS)

            def scores(n, it, g, s, h):
                half, i = STEPS[s]
                first, w = width(s)
                U = HG * (NS * n + s) + h
                if s == 0 and h == 0:
                    pe.wait_ge(max_loaded[g % 2], 48 * (group_pairs(it, g) + 1))
                pe.wait_ge(exp_done, U + 1)
                nc.tensor.matmul(ps_s[:, score_bank(s, h), :w], k_stack[:SR, g % STACKS, h, P * i:P * (i + 1)],
                                 q_stack[:SR, g % STACKS, h, first:first + w], start=True, stop=True).then_inc(scores_done, 1)

            def sums(n, g, s):
                half, i = STEPS[s]
                first, w = width(s)
                pe.wait_ge(exp_done, S_BANKS + HG * (NS * n + s + 1))
                if s in DIAGONAL:
                    pe.wait_ge(masked, len(DIAGONAL) * n + DIAGONAL.index(s) + 1)
                if i == 0:
                    pe.wait_ge(copied, 2 * n + half + 1)
                if s == 0:
                    pe.wait_ge(v_ready, n + 1)
                for h in range(HG):
                    last = nc.tensor.matmul(ps_o[VW * h:VW * (h + 1), first - SW * half:first - SW * half + w],
                                            v_ext[:, g % 2, i, h], prob[:, s % P_SETS, h, :w],
                                            start=(i == 0), stop=(s in (3, NS - 1)))
                last.then_inc(values_done, 1)

            def body(n, it, g, last):
                places = {}
                for r, at, slot in ring_units(it, g, last):
                    places.setdefault(RING_PLACE[r], []).append((r, at, slot))

                def ring_behind(place):
                    for r, at, slot in places.get(place, []):
                        ring(r, n, it, g, at, slot)
                for s in range(NS + LAG):
                    if s < NS:
                        for h in range(HG):
                            scores(n, it, g, s, h)
                            ring_behind((s, h))
                    if s >= LAG:
                        sums(n, g, s - LAG)
                        ring_behind((s, "sums"))
                ring_behind("end")
            rounds(pe, body)


def expert_phase(nc, m, a, slots_dram, y_dram):
    with ExitStack() as stack:
        sb = lambda name, shape, dt=F32: stack.enter_context(nc.sbuf_tensor(name, shape, dt))
        ps = lambda name, shape: stack.enter_context(nc.psum_tensor(name, shape, F32))
        w_hi, w_lo = sb("we_hi", [P, E, KC, WE], F32R), sb("we_lo", [P, E, KC, WE], F32R)
        more_raw = sb("we_raw_more", [P, RAW - EARLY, KC, WE])
        w_raw = [m["we_raw"][:, e] for e in range(EARLY)] + [more_raw[:, e] for e in range(RAW - EARLY)]
        x_in, y_out = sb("slot_in", [P, MOE_UNROLL, ROW]), sb("slot_out", [P, MOE_UNROLL, C])
        xt_hi, xt_lo, ht_hi, ht_lo = (sb(n, [P, 2, KC, P], F32R) for n in ("sx_hi", "sx_lo", "sh_hi", "sh_lo"))
        gate, clipped, inner = (sb(n, [P, 2, I]) for n in ("gate", "clipped", "inner"))
        ps_xt, ps_gu, ps_ht, ps_y = (ps(n, [P, 2, 512]) for n in ("ps_sx", "ps_gu", "ps_sh", "ps_y"))
        (w_hi_ready, w_lo_ready, x_turned, x_hi, x_lo, gu_done, gate_ready, clip_ready, inner_ready, h_turned,
         h_hi, h_lo, y_done, y_copied) = semaphores(
            nc, stack, "we_hi_ready we_lo_ready x_turned x_hi x_lo gu_done gate_ready clip_ready inner_ready "
            "h_turned h_hi h_lo y_done y_copied")
        w_loaded = m["we_loaded"]
        x_loaded = semaphores(nc, stack, " ".join(f"slot_loaded_{r}" for r in range(MOE_UNROLL)))
        y_sent = semaphores(nc, stack, " ".join(f"slot_sent_{r}" for r in range(MOE_UNROLL)))
        block = stack.enter_context(nc.Block())
        x_view = slots_dram.rearrange("(k p) c -> p k c", p=P)
        ROUNDS = MOE_TILES // MOE_UNROLL
        TURN, GU, HT, DOWN = 1, 2, 3, 4

        def rounds(engine, body):
            body(0, lambda k: 0 <= k)
            with engine.Fori(1, ROUNDS) as it:
                body(it, lambda k: True)
            body(ROUNDS, lambda k: k < MOE_TILES)

        def tiles(it, valid):
            for r in range(MOE_UNROLL):
                k = MOE_UNROLL * it + r
                ok = (lambda back, k=k: valid(k - back) if isinstance(k, int) else True)
                yield k, r, ok

        @block.sync
        def _(sp):
            for e in range(EARLY, E):
                wait(sp, w_lo_ready, e - RAW + 1)
                load_expert(sp, a, e, w_raw[e % RAW], w_loaded[e % RAW])

            def body(it, valid):
                for k, r, ok in tiles(it, valid):
                    if ok(0):
                        wait(sp, y_sent[r], 16 * it)
                        sp.dma_start(x_in[:, r:r + 1], x_view[:, bass.ds(k, 1)]).then_inc(x_loaded[r], 16)
            rounds(sp, body)

        @block.scalar
        def _(act):
            for e in range(E):
                act.wait_ge(w_loaded[e % RAW], 48 * (e // RAW + 1))
                nc.scalar.activation(w_hi[:, e], w_raw[e % RAW], ACT.Copy).then_inc(w_hi_ready, 1)

            def body(it, valid):
                for k, r, ok in tiles(it, valid):
                    if ok(TURN):
                        j, q = k - TURN, (r - TURN) % 2
                        act.wait_ge(x_turned, j + 1)
                        wait(act, gu_done, j - 1)
                        nc.scalar.activation(xt_hi[:, q], ps_xt[:, q, :C].rearrange("p (c t) -> p c t", c=KC),
                                             ACT.Copy).then_inc(x_hi, 1)
                    if ok(GU):
                        j, q = k - GU, (r - GU) % 2
                        act.wait_ge(gu_done, j + 1)
                        wait(act, clip_ready, j - 1)
                        nc.scalar.activation(gate[:, q], ps_gu[:, q, :I], ACT.Silu).then_inc(gate_ready, 1)
                    if ok(HT):
                        j, q = k - HT, (r - HT) % 2
                        act.wait_ge(h_turned, j + 1)
                        wait(act, y_done, j - 1)
                        nc.scalar.activation(ht_hi[:, q], ps_ht[:, q, :C].rearrange("p (c t) -> p c t", c=KC),
                                             ACT.Copy).then_inc(h_hi, 1)
                    if ok(DOWN):
                        j, q, rj = k - DOWN, (r - DOWN) % 2, (r - DOWN) % MOE_UNROLL
                        act.wait_ge(y_done, j + 1)
                        wait(act, y_sent[rj], 16 * (it - (r < DOWN)))
                        nc.scalar.activation(y_out[:, rj], ps_y[:, q, :C], ACT.Copy).then_inc(y_copied, 1)
            rounds(act, body)

        @block.gpsimd
        def _(pool):
            def body(it, valid):
                for k, r, ok in tiles(it, valid):
                    if ok(GU):
                        j, q = k - GU, (r - GU) % 2
                        wait_alone(pool, gate_ready, j + 1, m["passed"])
                        wait_alone(pool, inner_ready, j - 1, m["passed"])
                        nc.gpsimd.tensor_scalar(clipped[:, q], gate[:, q], LIMIT, -LIMIT, ALU.min, ALU.max).then_inc(clip_ready, 1)
                    if ok(DOWN + 1):
                        j, rj = k - DOWN - 1, (r - DOWN - 1) % MOE_UNROLL
                        wait_alone(pool, y_copied, j + 1, m["passed"])
                        nc.gpsimd.indirect_dma_start(
                            y_dram, bass.IndirectOffsetOnAxis(ap=x_in[:, rj, C:].bitcast(U32), axis=0),
                            y_out[:, rj], None).then_inc(y_sent[rj], 16)
            rounds(pool, body)
            for r in range(MOE_UNROLL):
                pool.wait_ge(y_sent[r], 16 * ROUNDS)

        @block.vector
        def _(dve):
            for e in range(E):
                dve.wait_ge(w_hi_ready, e + 1)
                nc.vector.tensor_tensor(w_lo[:, e], w_raw[e % RAW], w_hi[:, e].bitcast(F32), ALU.subtract).then_inc(w_lo_ready, 1)

            def body(it, valid):
                for k, r, ok in tiles(it, valid):
                    if ok(TURN):
                        j, q = k - TURN, (r - TURN) % 2
                        dve.wait_ge(x_hi, j + 1)
                        nc.vector.tensor_tensor(xt_lo[:, q], ps_xt[:, q, :C].rearrange("p (c t) -> p c t", c=KC),
                                                xt_hi[:, q].bitcast(F32), ALU.subtract).then_inc(x_lo, 1)
                    if ok(HT):
                        j, q = k - HT, (r - HT) % 2
                        dve.wait_ge(h_hi, j + 1)
                        nc.vector.tensor_tensor(ht_lo[:, q], ps_ht[:, q, :C].rearrange("p (c t) -> p c t", c=KC),
                                                ht_hi[:, q].bitcast(F32), ALU.subtract).then_inc(h_lo, 1)
                    if ok(GU):
                        j, q = k - GU, (r - GU) % 2
                        dve.wait_ge(clip_ready, j + 1)
                        wait(dve, h_turned, j - 1)
                        nc.vector.tensor_tensor(inner[:, q], ps_gu[:, q, I:], clipped[:, q], ALU.mult).then_inc(inner_ready, 1)
            rounds(dve, body)

        @block.tensor
        def _(pe):
            pe.wait_ge(w_lo_ready, E)

            def body(it, valid):
                first = max(MOE_UNROLL * it - DOWN, 0) if isinstance(it, int) else MOE_UNROLL * it - DOWN
                count = min(MOE_UNROLL * it + MOE_UNROLL - GU, MOE_TILES) - first if isinstance(it, int) else MOE_UNROLL + DOWN - GU
                _, experts = nc.values_load_multi_w_load_instructions(
                    m["owner"][0:1, bass.ds(first, count)], engines=[mybir.EngineType.PE], min_val=0, max_val=E - 1,
                    skip_runtime_bounds_check_because="it counts seven comparisons")
                back = 0 if isinstance(it, int) and it == 0 else DOWN
                for k, r, ok in tiles(it, valid):
                    if ok(TURN):
                        j, q, rj = k - TURN, (r - TURN) % 2, (r - TURN) % MOE_UNROLL
                        pe.wait_ge(x_loaded[rj], 16 * (it + 1 - (r < TURN)))
                        wait(pe, x_lo, j - 1)
                        for c in range(KC):
                            last = nc.tensor.transpose(ps_xt[:, q, c * P:(c + 1) * P], x_in[:, rj, c * P:(c + 1) * P], m["ident"][:])
                        last.then_inc(x_turned, 1)
                    if ok(GU):
                        j, q = k - GU, (r - GU) % 2
                        e = experts[r - GU + back]
                        pe.wait_ge(x_lo, j + 1)
                        wait(pe, inner_ready, j - 1)
                        terms = [(w, v, c) for c in range(KC) for w, v in ((w_hi, xt_hi), (w_hi, xt_lo), (w_lo, xt_hi))]
                        for i, (w, v, c) in enumerate(terms):
                            last = nc.tensor.matmul(ps_gu[:, q], v[:, q, c], w[:, e, c, :2 * I], start=(i == 0), stop=(i == len(terms) - 1))
                        last.then_inc(gu_done, 1)
                    if ok(HT):
                        j, q = k - HT, (r - HT) % 2
                        pe.wait_ge(inner_ready, j + 1)
                        wait(pe, h_lo, j - 1)
                        for c in range(KC):
                            last = nc.tensor.transpose(ps_ht[:, q, c * P:(c + 1) * P], inner[:, q, c * P:(c + 1) * P], m["ident"][:])
                        last.then_inc(h_turned, 1)
                    if ok(DOWN):
                        j, q = k - DOWN, (r - DOWN) % 2
                        e = experts[r - DOWN + back]
                        pe.wait_ge(h_lo, j + 1)
                        wait(pe, y_copied, j - 1)
                        terms = [(w, v, c) for c in range(KC) for w, v in ((w_hi, ht_hi), (w_hi, ht_lo), (w_lo, ht_hi))]
                        for i, (w, v, c) in enumerate(terms):
                            last = nc.tensor.matmul(ps_y[:, q, :C], v[:, q, c], w[:, e, c, 2 * I:], start=(i == 0), stop=(i == len(terms) - 1))
                        last.then_inc(y_done, 1)
            rounds(pe, body)


def output_phase(nc, m, x, y_dram, out):
    with ExitStack() as stack:
        sb = lambda name, shape, dt=F32: stack.enter_context(nc.sbuf_tensor(name, shape, dt))
        ps = lambda name, shape: stack.enter_context(nc.psum_tensor(name, shape, F32))
        RU = 4
        x_in, biased, heads, both, first, two, result = (sb(n, [P, RU, C]) for n in (
            "res_in", "biased", "heads", "both", "first_y", "two", "result"))
        y_in = sb("y_in", [P, RU, 2, C])
        a_hi, a_lo = (sb(n, [P, 2, KC, P], F32R) for n in ("a_hi", "a_lo"))
        ps_at, ps_z = (ps(n, [P, 2, 512]) for n in ("ps_at", "ps_z"))
        (heads_ready, turned, hi_ready, lo_ready, projected, biased_ready, both_ready, first_ready, two_ready,
         result_ready) = semaphores(nc, stack, "heads_ready heads_turned a_hi_ready a_lo_ready projected biased_ready "
                                    "both_ready first_ready two_ready result_ready")
        loaded = semaphores(nc, stack, " ".join(f"tile_loaded_{r}" for r in range(RU)))
        stored = semaphores(nc, stack, " ".join(f"out_stored_{r}" for r in range(RU)))
        block = stack.enter_context(nc.Block())
        x_view = x.rearrange("b (j p) c -> p (b j) c", p=P)
        y_view = y_dram[:2 * B * T].rearrange("(t p w) c -> p t w c", p=P, w=2)
        out_view = out.rearrange("b (j p) c -> p (b j) c", p=P)
        WO = 3 * C + E
        LOADED = 32

        def rounds(engine, body):
            body(0)
            with engine.Fori(1, TILES // RU) as it:
                body(it)

        def tiles(it):
            for r in range(RU):
                yield RU * it + r, r

        @block.sync
        def _(sp):
            def body(it):
                for t, r in tiles(it):
                    wait(sp, result_ready, t - RU + 1)
                    sp.dma_start(x_in[:, r:r + 1], x_view[:, bass.ds(t, 1)]).then_inc(loaded[r], 16)
                    sp.dma_start(y_in[:, r:r + 1], y_view[:, bass.ds(t, 1)]).then_inc(loaded[r], 16)
                    if not isinstance(t, int) or t >= RU - 1:
                        store(t - RU + 1, (r + 1) % RU)

            def store(t, r):
                sp.wait_ge(result_ready, t + 1)
                sp.dma_start(out_view[:, bass.ds(t, 1)], result[:, r:r + 1]).then_inc(stored[r], 16)
            rounds(sp, body)
            for t in range(TILES - RU + 1, TILES):
                store(t, t % RU)
            for r in range(RU):
                sp.wait_ge(stored[r], 16 * TILES // RU)

        @block.gpsimd
        def _(pool):
            def finish(t, r, it):
                wait_alone(pool, two_ready, t + 1, m["passed"])
                pool.wait_ge(first_ready, t + 1)
                wait(pool, stored[r], 16 * it)
                nc.gpsimd.tensor_tensor(result[:, r], two[:, r], first[:, r], ALU.add).then_inc(result_ready, 1)

            def body(it):
                for t, r in tiles(it):
                    wait_alone(pool, loaded[r], LOADED * (it + 1), m["passed"])
                    wait(pool, both_ready, t - RU + 1)
                    nc.gpsimd.tensor_tensor(biased[:, r], x_in[:, r], m["row_bias"][:, 1], ALU.add).then_inc(biased_ready, 1)
                    if r or not isinstance(it, int):
                        finish(t - 1, (r - 1) % RU, it if r else it - 1)
            rounds(pool, body)
            finish(TILES - 1, RU - 1, TILES // RU - 1)

        @block.scalar
        def _(act):
            def body(it):
                for t, r in tiles(it):
                    wait(act, turned, t - RU + 1)
                    nc.scalar.activation(heads[:, r].rearrange("p (g c) -> p g c", g=NG), m["attn"][:, :, t],
                                         ACT.Copy).then_inc(heads_ready, 1)
                    act.wait_ge(loaded[r], LOADED * (it + 1))
                    wait(act, result_ready, t - RU + 1)
                    nc.scalar.activation(first[:, r], y_in[:, r, 0], ACT.Copy,
                                         scale=m["weight"][:, 0, bass.ds(t, 1)]).then_inc(first_ready, 1)
                    act.wait_ge(turned, t + 1)
                    wait(act, projected, t - 1)
                    nc.scalar.activation(a_hi[:, r % 2], ps_at[:, r % 2, :C].rearrange("p (c t) -> p c t", c=KC),
                                         ACT.Copy).then_inc(hi_ready, 1)
            rounds(act, body)

        @block.vector
        def _(dve):
            def low(t, r):
                dve.wait_ge(hi_ready, t + 1)
                nc.vector.tensor_tensor(a_lo[:, r % 2], ps_at[:, r % 2, :C].rearrange("p (c t) -> p c t", c=KC),
                                        a_hi[:, r % 2].bitcast(F32), ALU.subtract).then_inc(lo_ready, 1)

            def add(t, r, it):
                dve.wait_ge(projected, t + 1)
                dve.wait_ge(biased_ready, t + 1)
                nc.vector.tensor_tensor(both[:, r], ps_z[:, r % 2, :C], biased[:, r], ALU.add).then_inc(both_ready, 1)
                dve.wait_ge(both_ready, t + 1)
                dve.wait_ge(loaded[r], LOADED * (it + 1))
                wait(dve, result_ready, t - RU + 1)
                nc.vector.scalar_tensor_tensor(out=two[:, r], in0=y_in[:, r, 1], scalar=m["weight"][:, 1, bass.ds(t, 1)],
                                               in1=both[:, r], op0=ALU.mult, op1=ALU.add).then_inc(two_ready, 1)

            def body(it):
                for t, r in tiles(it):
                    low(t, r)
                    if r or not isinstance(it, int):
                        add(t - 1, (r - 1) % RU, it if r else it - 1)
            rounds(dve, body)
            add(TILES - 1, RU - 1, TILES // RU - 1)

        @block.tensor
        def _(pe):
            terms = [(w, v, c) for c in range(KC) for w, v in ((m["w_hi"], a_hi), (m["w_hi"], a_lo), (m["w_lo"], a_hi))]

            def turn(t, r):
                pe.wait_ge(heads_ready, t + 1)
                wait(pe, lo_ready, t - 1)
                for c in range(KC):
                    last = nc.tensor.transpose(ps_at[:, r % 2, c * P:(c + 1) * P], heads[:, r, c * P:(c + 1) * P], m["ident"][:])
                last.then_inc(turned, 1)

            def project(t, r):
                pe.wait_ge(lo_ready, t + 1)
                wait(pe, both_ready, t - 1)
                for i, (w, v, c) in enumerate(terms):
                    last = nc.tensor.matmul(ps_z[:, r % 2, :C], v[:, r % 2, c], w[:, c, WO:WO + C], start=(i == 0), stop=(i == len(terms) - 1))
                last.then_inc(projected, 1)

            def body(it):
                for t, r in tiles(it):
                    turn(t, r)
                    if r or not isinstance(it, int):
                        project(t - 1, (r - 1) % RU)
            rounds(pe, body)
            project(TILES - 1, RU - 1)


def program(nc, a, out):
    xn_dram = nc.dram_tensor("xn_scratch", (B * T, C), F32, kind="Internal").ap()
    parts_dram = nc.dram_tensor("parts_scratch", (3, 2, B, C, T), BF16, kind="Internal").ap()
    slots_dram = nc.dram_tensor("slots_scratch", (MOE_TILES * P, ROW), F32, kind="Internal").ap()
    y_dram = nc.dram_tensor("y_scratch", (2 * B * T + MOE_TILES * P, C), F32, kind="Internal").ap()
    with ExitStack() as stack:
        shapes = {
            "w_hi": ([P, KC, 4 * C + E], F32R), "w_lo": ([P, KC, 4 * C + E], F32R),
            "qk_bias": ([P, 2, KC], F32), "row_bias": ([P, 2, C], F32), "eps": ([P, 1], F32),
            "ident": ([P, P], F32), "ident_b": ([P, P], BF16), "mask_b": ([P, P], BF16),
            "attn": ([P, NG, TILES, GC], F32), "logits": ([P, TILES, E], F32),
            "weight": ([P, 2, TILES], F32), "slot": ([P, 2, TILES], U32), "owner": ([P, MOE_TILES], U32),
            "token_row": ([P, TILES, 2], U32), "we_raw": ([P, EARLY, KC, WE], F32),
        }
        m = {n: stack.enter_context(nc.sbuf_tensor(n, sh, dt)) for n, (sh, dt) in shapes.items()}
        m["x_loaded"] = semaphores(nc, stack, "x_loaded_even x_loaded_odd")
        m["we_loaded"] = semaphores(nc, stack, " ".join(f"expert_loaded_{e}" for e in range(RAW)))
        m["passed"] = stack.enter_context(nc.semaphore("passed"))
        with ExitStack() as stack2:
            more = {"v_all": ([P, GROUPS, QT, GC], F32), "v_ext": ([P, 2, QT, HG, VW], F32),
                    "k_stack": ([P, STACKS, HG, T], BF16)}
            m.update({n: stack2.enter_context(nc.sbuf_tensor(n, sh, dt)) for n, (sh, dt) in more.items()})
            setup_phase(nc, m, a)
            project_phase(nc, m, a["x"], xn_dram, parts_dram, slots_dram)
            route_phase(nc, m)
            with ExitStack() as stack3:
                more = {"q_stack": ([P, STACKS, HG, T], BF16)}
                m.update({n: stack3.enter_context(nc.sbuf_tensor(n, sh, dt)) for n, (sh, dt) in more.items()})
                attention_phase(nc, m, a, parts_dram, xn_dram, slots_dram)
        expert_phase(nc, m, a, slots_dram, y_dram)
        output_phase(nc, m, a["x"], y_dram, out)


NAMES = {"x": "L0_attn_idx", "Wq": "L0_attn_Wq", "bq": "L0_attn_bq", "Wk": "L0_attn_Wk", "bk": "L0_attn_bk",
         "Wv": "L0_attn_Wv", "bv": "L0_attn_bv", "Wo": "L0_attn_Wo", "bo": "L0_attn_bo", "Wr": "L0_ffn_Wr",
         "Wg": "L0_ffn_Wg", "Wu": "L0_ffn_Wu", "Wd": "L0_ffn_Wd"}


def kernel(**inputs):
    import concourse.bacc as bacc
    from concourse.bass_utils import run_bass_kernel_spmd

    nc = bacc.Bacc("TRN2", target_bir_lowering=False, num_devices=1)
    arrays, a = {}, {}
    for short, name in NAMES.items():
        v = np.ascontiguousarray(inputs[name])
        arrays[f"in_{short}"] = v
        a[short] = nc.dram_tensor(f"in_{short}", v.shape, mybir.dt.from_np(v.dtype), kind="ExternalInput").ap()
    out = nc.dram_tensor("out", (B, T, C), F32, kind="ExternalOutput").ap()
    program(nc, a, out)
    return run_bass_kernel_spmd(nc, [arrays], core_ids=[0]).results[0]["out"]
```
